# Optimizing a Trainium2 kernel written in Bass

```python
import numpy as np
import jax
import jax.numpy as jnp

def _softmax(x, axis=-1):
    return jax.nn.softmax(x, axis=axis)

def _gelu(x):
    return jax.nn.gelu(x, approximate=True)

def _silu(x):
    return jax.nn.silu(x)

def _sigmoid(x):
    return jax.nn.sigmoid(x)

def _layernorm(x, axis=-1, eps=1e-05):
    m = jnp.mean(x, axis=axis, keepdims=True)
    v = jnp.var(x, axis=axis, keepdims=True)
    return (x - m) / jnp.sqrt(v + eps)

def _scatter_add(tgt, idx, src, axis=0):
    return tgt.at[idx].add(src)

def _segment_sum(src, seg, n):
    return jax.ops.segment_sum(src, seg, n)
kernel_name = 'mk_seq_preln_d1_jaxref_r8_1aa4ef'

def setup_inputs(seed: int=0):
    np.random.seed(seed)
    _w = jnp.asarray

    def _L0_attn_setup():
        import jax, jax.numpy as jnp
        import numpy as np
        B, S, D = (2, 256, 256)
        N_HEADS, N_KV_HEADS = (16, 4)
        HEAD_DIM = D // N_HEADS

        def _apply_rope(xh, positions):
            Dh = xh.shape[-1]
            half = Dh // 2
            freqs = 1.0 / 10000.0 ** (jnp.arange(half, dtype=jnp.float32) / half)
            angles = positions[:, None].astype(jnp.float32) * freqs[None, :]
            cos, sin = (jnp.cos(angles), jnp.sin(angles))
            xp = xh.reshape(*xh.shape[:-1], half, 2)
            x0, x1 = (xp[..., 0], xp[..., 1])
            r0 = x0 * cos - x1 * sin
            r1 = x0 * sin + x1 * cos
            return jnp.stack([r0, r1], axis=-1).reshape(xh.shape)
        key = jax.random.key(seed)
        ks = jax.random.split(key, 5)
        x = jax.random.normal(ks[0], (B, S, D), dtype=jnp.float32)
        W_q = jax.random.normal(ks[1], (D, D), dtype=jnp.float32) * 0.02
        W_k = jax.random.normal(ks[2], (D, N_KV_HEADS * HEAD_DIM), dtype=jnp.float32) * 0.02
        W_v = jax.random.normal(ks[3], (D, N_KV_HEADS * HEAD_DIM), dtype=jnp.float32) * 0.02
        W_o = jax.random.normal(ks[4], (D, D), dtype=jnp.float32) * 0.02
        return {'x': x, 'W_q': W_q, 'W_k': W_k, 'W_v': W_v, 'W_o': W_o}
    _L0_attn_in = _L0_attn_setup()

    def _L0_ffn_setup():
        import jax, jax.numpy as jnp
        import numpy as np
        D_MODEL = 256
        HIDDEN = int(2 * D_MODEL * 4 / 3)

        def ternary_quant(w):
            s = jnp.mean(jnp.abs(w))
            q = jnp.clip(jnp.round(w / s), -1.0, 1.0) * s
            return w + jax.lax.stop_gradient(q - w)
        key = jax.random.key(seed)
        k0, k1, k2, k3 = jax.random.split(key, 4)
        x = jax.random.normal(k0, (4, 512, D_MODEL), dtype=jnp.float32)
        std_in = 1.0 / np.sqrt(D_MODEL)
        std_h = 1.0 / np.sqrt(HIDDEN)
        w1 = jax.random.uniform(k1, (HIDDEN, D_MODEL), jnp.float32, -std_in, std_in)
        w3 = jax.random.uniform(k2, (HIDDEN, D_MODEL), jnp.float32, -std_in, std_in)
        w2 = jax.random.uniform(k3, (D_MODEL, HIDDEN), jnp.float32, -std_h, std_h)
        return {'x': x, 'w1': w1, 'w3': w3, 'w2': w2}
    _L0_ffn_in = _L0_ffn_setup()
    _d = {'L0_attn_x': _L0_attn_in['x'], 'L0_attn_W_q': _L0_attn_in['W_q'], 'L0_attn_W_k': _L0_attn_in['W_k'], 'L0_attn_W_v': _L0_attn_in['W_v'], 'L0_attn_W_o': _L0_attn_in['W_o'], 'L0_ffn_w1': _L0_ffn_in['w1'], 'L0_ffn_w3': _L0_ffn_in['w3'], 'L0_ffn_w2': _L0_ffn_in['w2']}
    _x0 = _d['L0_attn_x']
    _d['L0_attn_x'] = jax.random.normal(jax.random.fold_in(jax.random.key(seed), 1), (4, 256, 256), dtype=_x0.dtype)
    del _x0
    return _d

def reference(L0_attn_x, L0_attn_W_q, L0_attn_W_k, L0_attn_W_v, L0_attn_W_o, L0_ffn_w1, L0_ffn_w3, L0_ffn_w2):

    def _L0_attn_ref(x, W_q, W_k, W_v, W_o):
        import jax, jax.numpy as jnp
        import numpy as np
        B, S, D = (2, 256, 256)
        N_HEADS, N_KV_HEADS = (16, 4)
        HEAD_DIM = D // N_HEADS

        def _apply_rope(xh, positions):
            Dh = xh.shape[-1]
            half = Dh // 2
            freqs = 1.0 / 10000.0 ** (jnp.arange(half, dtype=jnp.float32) / half)
            angles = positions[:, None].astype(jnp.float32) * freqs[None, :]
            cos, sin = (jnp.cos(angles), jnp.sin(angles))
            xp = xh.reshape(*xh.shape[:-1], half, 2)
            x0, x1 = (xp[..., 0], xp[..., 1])
            r0 = x0 * cos - x1 * sin
            r1 = x0 * sin + x1 * cos
            return jnp.stack([r0, r1], axis=-1).reshape(xh.shape)
        b, s, d = x.shape
        positions = jnp.arange(s)
        rep = N_HEADS // N_KV_HEADS
        Q = (x @ W_q).reshape(b, s, N_HEADS, HEAD_DIM).transpose(0, 2, 1, 3)
        K = (x @ W_k).reshape(b, s, N_KV_HEADS, HEAD_DIM).transpose(0, 2, 1, 3)
        V = (x @ W_v).reshape(b, s, N_KV_HEADS, HEAD_DIM).transpose(0, 2, 1, 3)
        Qr = _apply_rope(Q, positions)
        K_rep = jnp.tile(K, (1, rep, 1, 1))
        V_rep = jnp.tile(V, (1, rep, 1, 1))
        Kr = _apply_rope(K_rep, positions)
        scores = jnp.einsum('bhqd,bhkd->bhqk', Qr, Kr) / HEAD_DIM ** 0.5
        weights = jax.nn.softmax(scores, axis=-1)
        out = jnp.einsum('bhqk,bhkd->bhqd', weights, V_rep)
        out = out.transpose(0, 2, 1, 3).reshape(b, s, d)
        return out @ W_o

    def _L0_ffn_ref(x, w1, w3, w2):
        import jax, jax.numpy as jnp
        import numpy as np
        D_MODEL = 256
        HIDDEN = int(2 * D_MODEL * 4 / 3)

        def ternary_quant(w):
            s = jnp.mean(jnp.abs(w))
            q = jnp.clip(jnp.round(w / s), -1.0, 1.0) * s
            return w + jax.lax.stop_gradient(q - w)
        w1q = ternary_quant(w1)
        w3q = ternary_quant(w3)
        w2q = ternary_quant(w2)
        h1 = jnp.einsum('bsd,hd->bsh', x, w1q)
        h3 = jnp.einsum('bsd,hd->bsh', x, w3q)
        g = jax.nn.silu(h1) * h3
        return jnp.einsum('bsh,dh->bsd', g, w2q)
    x = L0_attn_x
    x = x + _L0_attn_ref(_layernorm(x, axis=-1), L0_attn_W_q, L0_attn_W_k, L0_attn_W_v, L0_attn_W_o)
    x = x + _L0_ffn_ref(_layernorm(x, axis=-1), L0_ffn_w1, L0_ffn_w3, L0_ffn_w2)
    return x

_drawn_inputs = setup_inputs


def setup_inputs(seed=0):
    import zlib

    import numpy as np

    out = dict(_drawn_inputs(seed))
    spreads = {}
    factors = {'L0_attn_W_q': 8.0,
     'L0_attn_W_k': 8.0,
     'L0_attn_W_v': 8.0,
     'L0_attn_W_o': 8.0,
     'L0_ffn_w1': 6.838,
     'L0_ffn_w3': 6.662,
     'L0_ffn_w2': 6.673}
    for name, (base, spread) in spreads.items():
        noise = np.random.default_rng([zlib.crc32(name.encode()), seed]).standard_normal(out[name].shape)
        drawn = base * np.exp(spread * noise) if base else spread * noise
        out[name] = jnp.asarray(drawn.astype(out[name].dtype))
    for name, factor in factors.items():
        out[name] = (out[name] * factor).astype(out[name].dtype)
    return out
```

```python
from contextlib import ExitStack

import numpy as np

import concourse.bass as bass
from concourse import mybir

F32 = mybir.dt.float32
BF16 = mybir.dt.bfloat16
F16 = mybir.dt.float16
ALU = mybir.AluOpType
ACT = mybir.ActivationFunctionType
AX = mybir.AxisListType

P = 128
NB, S, D = 4, 256, 256
NT = NB * S // P
HD, NKV, REP = 16, 4, 4
NH = NKV * REP
NQK = NH + NKV
QKV = D + 2 * NKV * HD
KC = D // P
HID = int(2 * D * 4 / 3)
CH = 6
HC = 114
HP = CH * HC
LAST = HID - (CH - 1) * HC
SLOT = 6 * HD
MROW = 3
EPS = 1e-5
GT = 512
NG = NB * S // GT
W3SHIFT = 2.0 ** -6
VW = 32


def build(nc, x, wqkv, wo, w1, w3, w2, consts, out):
    ctx = ExitStack()
    with ctx:
        def sb(name, shape, dt=F32):
            return ctx.enter_context(nc.sbuf_tensor(name, shape, dt))

        def sem(name):
            return ctx.enter_context(nc.semaphore(name))

        x_sb = sb("x_sb", [P, NT, D])
        x1 = sb("x1", [P, NT, D])
        wqkv_sb = sb("wqkv_sb", [P, KC, QKV])
        wo_sb = sb("wo_sb", [P, KC, D])
        cst = sb("cst", [P, P + 4 * HD])
        id32 = cst[:, 0:P]
        cos = cst[:, P:P + 2 * HD].rearrange("p (q d) -> p q d", q=2)
        sin = cst[:, P + 2 * HD:P + 4 * HD].rearrange("p (q d) -> p q d", q=2)
        idb = sb("idb", [P, P], BF16)
        idh = sb("idh", [P, P], F16)
        ones = sb("ones", [P, P])
        mhalf = sb("mhalf", [P, 2])
        st1 = sb("st1", [P, NT, 6])
        mv1 = sb("mv1", [P, NT, 2])
        rs1 = sb("rs1", [P, NT, 2])
        hn = sb("hn", [P, NT, D])
        hT = sb("hT", [P, 2, KC, P])
        ra = sb("ra", [P, 4, NQK * HD])
        rb = sb("rb", [P, 4, NQK * HD])
        rq = sb("rq", [P, 4, NQK * HD])
        r1 = sb("r1", [P, 4, NQK * HD])
        part = sb("part", [P, 4, NQK, 6, HD], BF16)
        vst = sb("vst", [P, NT, NKV, VW])
        qs = sb("qs", [P, 2, NH, S], BF16)
        ks = sb("ks", [P, 2, NKV, S], BF16)
        nmx = sb("nmx", [P, 2, NH])
        nmr = sb("nmr", [P, 2, NH])
        nms = sb("nms", [P, 2, MROW, NH], BF16)
        nmT = sb("nmT", [MROW * NH, 2, S], BF16)
        pt = sb("pt", [P, 3, REP, S])
        ot = sb("ot", [P, NKV, S])
        rden = sb("rden", [P, 2, NH])
        on = sb("on", [P, 2, REP, NKV, HD])
        oT = sb("oT", [P, 2, KC, P])
        st2 = sb("st2", [P, NT, 6])
        mv2 = sb("mv2", [P, NT, 2])
        rs2 = sb("rs2", [P, NT, 2])
        h2 = sb("h2", [P, 2, D])
        h2T = sb("h2T", [P, 2, KC, NB * S], F16)
        w1n = sb("w1n", [HC, CH, D])
        w3n = sb("w3n", [HC, CH, D])
        w2n = sb("w2n", [P, KC, HP])
        tern = sb("tern", [P, 3, CH * D], F16)
        tpos = sb("tpos", [P, CH * D], F16)
        wabs = sb("wabs", [P, CH * D], BF16)
        wsum = sb("wsum", [P, 3])
        scl = sb("scl", [P, 3])
        thr = sb("thr", [P, 3])
        nthr = sb("nthr", [P, 3])
        sgate = sb("sgate", [P, 1])
        sout = sb("sout", [P, 2])
        w1T = sb("w1T", [P, KC, HP], F16)
        w3T = sb("w3T", [P, KC, HP], F16)
        w2T = sb("w2T", [HC, CH, D], F16)
        u = sb("u", [HC, 2, GT])
        uv = sb("uv", [HC, 2, GT])
        g = sb("g", [HC, 2, GT])
        gT = sb("gT", [HC, 2, CH, GT], F16)
        y = sb("y", [P, 2, D])

        ps = ctx.enter_context(nc.psum_tensor("ps", [P, 8, 512], F32))

        def bank(i, n=512):
            return ps[:, i, 0:n]

        in_x = [sem(f"in_x{b}") for b in range(NB)]
        in_cst, in_wqkv, in_wo = sem("in_cst"), sem("in_wqkv"), sem("in_wo")
        in_w = [sem(f"in_w{i}") for i in range(3)]
        pool_init, dve_pad, idents = sem("pool_init"), sem("dve_pad"), sem("idents")
        dve_step, pool_step, act_step = sem("dve_step"), sem("pool_step"), sem("act_step")
        var1, rstd1, normed1 = sem("var1"), sem("rstd1"), sem("normed1")
        hT_psum, hT_ready, qkv_psum = sem("hT_psum"), sem("hT_ready"), sem("qkv_psum")
        rope_prod, v_ready, roped = sem("rope_prod"), sem("v_ready"), sem("roped")
        p0k_ready, p1k_ready = sem("p0k_ready"), sem("p1k_ready")
        p0_ready, r1_ready, p1_ready, parts_ready = sem("p0_ready"), sem("r1_ready"), sem("p1_ready"), sem("parts_ready")
        stack_psum, stack_act, stack_dve = sem("stack_psum"), sem("stack_act"), sem("stack_dve")
        max_psum, max_done, nms_ready = sem("max_psum"), sem("max_done"), sem("nms_ready")
        nmT_psum, nmT_ready, mrows = sem("nmT_psum"), sem("nmT_ready"), sem("mrows")
        score_psum, exp_done, pv_done = sem("score_psum"), sem("exp_done"), sem("pv_done")
        ot_ready, o_psum, on_ready = sem("ot_ready"), sem("o_psum"), sem("on_ready")
        oT_psum, oT_ready, wo_psum, x1_ready = sem("oT_psum"), sem("oT_ready"), sem("wo_psum"), sem("x1_ready")
        var2, rstd2, h2_ready, h2T_psum = sem("var2"), sem("rstd2"), sem("h2_ready"), sem("h2T_psum")
        h2hi, h2lo = sem("h2hi"), sem("h2lo")
        wsum_ready, wtot_psum, scale_ready, tern_ready = sem("wsum_ready"), sem("wtot_psum"), sem("scale_ready"), sem("tern_ready")
        wT_psum, wT_ready = sem("wT_psum"), sem("wT_ready")
        up_psum, tanh_done, g_ready, ghi, glo = sem("up_psum"), sem("tanh_done"), sem("g_ready"), sem("ghi"), sem("glo")
        down_psum, y_ready, stored = sem("down_psum"), sem("y_ready"), [sem(f"stored{i}") for i in range(2)]

        block = ctx.enter_context(nc.Block())

        @block.sync
        def _(sp):
            def load_x(b):
                sp.dma_start(x_sb[:, 2 * b:2 * b + 2, :],
                             x[b].rearrange("(t p) d -> p t d", p=P)).then_inc(in_x[b], 16)

            load_x(0)
            sp.dma_start(cst[:, :], consts).then_inc(in_cst, 16)
            for i, w in enumerate(wqkv):
                n0 = (0, D, D + NKV * HD)[i]
                sp.dma_start(wqkv_sb[:, :, n0:n0 + w.shape[1]],
                             w.rearrange("(k p) n -> p k n", p=P)).then_inc(in_wqkv, 16)
            for b in range(1, NB):
                load_x(b)
            sp.dma_start(wo_sb[:, :, :], wo.rearrange("(k p) n -> p k n", p=P)).then_inc(in_wo, 16)
            sp.wait_ge(dve_pad, 3)
            for i, (w, wn) in enumerate(((w1, w1n), (w3, w3n))):
                sp.dma_start(wn[:, 0:CH - 1, :],
                             w[0:(CH - 1) * HC, :].rearrange("(c p) d -> p c d", p=HC)).then_inc(in_w[i], 16)
                sp.dma_start(wn[0:LAST, CH - 1, :], w[(CH - 1) * HC:HID, :]).then_inc(in_w[i], 16)
            sp.dma_start(w2n[:, :, 0:HID], w2.rearrange("(k p) h -> p k h", p=P)).then_inc(in_w[2], 16)

            def max_rows(b):
                sp.wait_ge(nmT_ready, b + 1)
                for m in range(MROW):
                    sp.dma_start(qs[SLOT + m:SLOT + m + 1, b % 2, :, :],
                                 nmT[m * NH:(m + 1) * NH, b % 2, :]).then_inc(mrows, 16)

            for b in range(NB):
                max_rows(b)
            for t in range(NT):
                sp.wait_ge(y_ready, t + 1)
                sp.dma_start(out[t // 2, (t % 2) * P:(t % 2 + 1) * P, :], y[:, t % 2, :]).then_inc(stored[t % 2], 16)
            for i in range(2):
                sp.wait_ge(stored[i], 16 * (NT // 2))

        @block.gpsimd
        def _(pool):
            for n, (dst, value) in enumerate(((mhalf[:, :], -0.5), (vst[:, :, :, :], 0.0),
                                              (vst[:, :, :, HD:HD + 1], 1.0),
                                              (ks[SLOT:SLOT + MROW, :, :, :], 1.0), (ones[:, :], 1.0))):
                nc.gpsimd.memset(dst, value).then_inc(pool_init, 1)
                pool.wait_ge(pool_init, n + 1)
            steps = [0]

            def chain(ins):
                steps[0] += 1
                ins.then_inc(pool_step, 1)
                pool.wait_ge(pool_step, steps[0])

            def rsqrt(rs, var, b):
                sl = slice(2 * b, 2 * b + 2)
                chain(nc.gpsimd.tensor_scalar(rs[:, sl, 0], var[:, sl, 1], EPS, None, ALU.add))
                return nc.gpsimd.tensor_tensor(rs[:, sl, 1], rs[:, sl, 0], mhalf[:, :], ALU.pow)

            def rsqrt1(b):
                pool.wait_ge(var1, b + 1)
                rsqrt(rs1, mv1, b).then_inc(rstd1, 1)

            def rsqrt2(b):
                pool.wait_ge(var2, b + 1)
                rsqrt(rs2, mv2, b).then_inc(rstd2, 1)

            def split(t):
                i = t % 4
                q, k = part[:, i, 0:NH], part[:, i, NH:NQK]
                heads = lambda a: a[:, i].rearrange("p (h d) -> p h d", d=HD)
                pool.wait_ge(rope_prod, t + 1)
                nc.gpsimd.tensor_tensor(rq[:, i], ra[:, i], rb[:, i], ALU.add).then_inc(roped, 1)
                pool.wait_ge(roped, t + 1)
                nc.gpsimd.tensor_copy(k[:, :, 1:6:2, :], heads(rq)[:, NH:NQK].unsqueeze(2).broadcast_to([P, NKV, 3, HD])
                                      ).then_inc(p0k_ready, 1)
                pool.wait_ge(p0k_ready, t + 1)
                pool.wait_ge(p0_ready, t + 1)
                nc.gpsimd.tensor_tensor(heads(r1), heads(rq), part[:, i, :, 1, :], ALU.subtract).then_inc(r1_ready, 1)
                pool.wait_ge(r1_ready, t + 1)
                nc.gpsimd.tensor_copy(k[:, :, 0:5:4, :], heads(r1)[:, NH:NQK].unsqueeze(2).broadcast_to([P, NKV, 2, HD])
                                      ).then_inc(p1k_ready, 1)
                pool.wait_ge(p1k_ready, t + 1)
                nc.gpsimd.tensor_tensor(k[:, :, 2, :], heads(r1)[:, NH:NQK], k[:, :, 4, :], ALU.subtract
                                        ).then_inc(parts_ready, 1)
                pool.wait_ge(p1_ready, t + 1)
                nc.gpsimd.tensor_tensor(q[:, :, 5, :], heads(r1)[:, 0:NH], q[:, :, 4, :], ALU.subtract
                                        ).then_inc(parts_ready, 1)

            rsqrt1(0)
            rsqrt1(1)
            split(0)
            split(1)
            rsqrt1(2)
            rsqrt1(3)
            split(2)
            split(3)
            for b in range(NB):
                if b >= 1:
                    rsqrt2(b - 1)
                if b + 2 < NB:
                    split(2 * b + 4)
                    split(2 * b + 5)
            rsqrt2(NB - 1)

        @block.scalar
        def _(act):
            act.wait_ge(in_cst, 16)
            nc.scalar.activation(idb[:, :], id32, ACT.Copy).then_inc(idents, 1)
            nc.scalar.activation(idh[:, :], id32, ACT.Copy).then_inc(idents, 1)

            def evac_hT(t):
                act.wait_ge(hT_psum, t + 1)
                nc.scalar.activation(hT[:, t % 2].rearrange("p k n -> p (k n)"), bank(2 + t % 2, D), ACT.Copy).then_inc(hT_ready, 1)

            def evac_v(t):
                act.wait_ge(qkv_psum, t + 1)
                act.wait_ge(rope_prod, t + 1)
                if t == 0:
                    act.wait_ge(pool_init, 3)
                nc.scalar.activation(vst[:, t, :, 0:HD],
                                     bank(6 + t % 2)[:, NQK * HD:QKV].rearrange("p (k d) -> p k d", d=HD),
                                     ACT.Copy).then_inc(v_ready, 1)

            def split0(t):
                act.wait_ge(roped, t + 1)
                src = rq[:, t % 4, 0:NH * HD].rearrange("p (h d) -> p h d", d=HD).unsqueeze(2)
                nc.scalar.activation(part[:, t % 4, 0:NH, 0:3, :], src.broadcast_to([P, NH, 3, HD]),
                                     ACT.Copy).then_inc(p0_ready, 1)

            def split1(t):
                act.wait_ge(r1_ready, t + 1)
                src = r1[:, t % 4, 0:NH * HD].rearrange("p (h d) -> p h d", d=HD).unsqueeze(2)
                nc.scalar.activation(part[:, t % 4, 0:NH, 3:5, :], src.broadcast_to([P, NH, 2, HD]),
                                     ACT.Copy).then_inc(p1_ready, 1)

            def evac_q(b, i):
                act.wait_ge(stack_psum, 5 * b + i + 1)
                half, qt = i % 2, i // 2
                nc.scalar.activation(qs[0:SLOT, b % 2, 8 * half:8 * half + 8, qt * P:(qt + 1) * P],
                                     ps[0:SLOT, i, :].bitcast(BF16).rearrange("p (h n) -> p h n", n=P),
                                     ACT.Copy).then_inc(stack_act, 1)

            def evac_oT(b, qt):
                act.wait_ge(oT_psum, 2 * b + qt + 1)
                nc.scalar.activation(oT[:, qt].rearrange("p k n -> p (k n)"), bank(4 + qt, D), ACT.Copy).then_inc(oT_ready, 1)

            def evac_ot(b, half):
                act.wait_ge(pv_done, 8 * b + 4 * half + 4)
                if b >= 1 and half == 0:
                    act.wait_ge(o_psum, 2 * b)
                nc.scalar.activation(ot[:, 2 * half:2 * half + 2, :].rearrange("p k s -> p (k s)"),
                                     bank(6), ACT.Copy).then_inc(ot_ready, 1)

            def exps(b, v):
                n = 8 * b + v
                act.wait_ge(score_psum, n + 1)
                if n >= 3:
                    act.wait_ge(pv_done, n - 2)
                src = ps[:, 2 * (n % 2):2 * (n % 2) + 2, :].rearrange("p a s -> p (a s)")
                nc.scalar.activation(pt[:, n % 3].rearrange("p r s -> p (r s)"), src, ACT.Exp,
                                     scale=float(HD) ** -0.5).then_inc(exp_done, 1)

            def split_h2(b, qt):
                t = 2 * b + qt
                act.wait_ge(h2T_psum, t + 1)
                nc.scalar.activation(h2T[:, 0, :, t * P:(t + 1) * P],
                                     bank(7, D).rearrange("p (k n) -> p k n", k=KC), ACT.Copy).then_inc(h2hi, 1)

            def weight_sums():
                for i, wn in enumerate((w1n, w3n, w2n)):
                    n = HC if i < 2 else P
                    act.wait_ge(in_w[i], 32 if i < 2 else 16)
                    if i == 0:
                        act.wait_ge(dve_pad, 5)
                    else:
                        act.wait_ge(act_step, i)
                    src = wn[:, :, :].rearrange("p c d -> p (c d)")
                    m = src.shape[1]
                    nc.scalar.activation(wabs[0:n, 0:m], src, ACT.Abs,
                                         accum_out=wsum[0:n, i:i + 1]).then_inc(act_step, 1)
                act.wait_ge(act_step, 3)
                nc.scalar.activation(idh[:, :], idb[:, :], ACT.Copy).then_inc(wsum_ready, 1)

            evac_hT(0)
            evac_hT(1)
            for t in range(2):
                evac_v(t)
                split0(t)
                split1(t)
            evac_hT(2)
            evac_hT(3)
            evac_q(0, 0)
            evac_q(0, 2)
            for t in range(2, 4):
                evac_v(t)
                split0(t)
                split1(t)
            evac_q(1, 0)
            evac_q(1, 2)
            weight_sums()
            for b in range(NB):
                t = 2 * b + 4
                if t < NT:
                    evac_hT(t)
                    evac_hT(t + 1)
                if b >= 1:
                    evac_oT(b - 1, 0)
                    evac_oT(b - 1, 1)
                for v in range(8):
                    exps(b, v)
                    if t < NT:
                        if v == 0:
                            evac_v(t)
                        if v == 1:
                            evac_v(t + 1)
                            split0(t)
                        if v == 2:
                            split1(t)
                        if v == 3:
                            split0(t + 1)
                        if v == 5:
                            split1(t + 1)
                    if v == 4:
                        evac_ot(b, 0)
                    if b >= 1 and v == 5:
                        split_h2(b - 1, 0)
                    if b >= 1 and v == 7:
                        split_h2(b - 1, 1)
                evac_ot(b, 1)
                if b + 2 < NB:
                    evac_q(b + 2, 0)
                    evac_q(b + 2, 2)
            evac_oT(NB - 1, 0)
            evac_oT(NB - 1, 1)
            for i in range(6):
                act.wait_ge(wT_psum, i + 1)
                k = i % 2
                if i < 4:
                    dst = (w1T, w3T)[i // 2][:, k, :]
                    src = bank(4 + k).bitcast(F16)[:, 0:HP]
                    nc.scalar.activation(dst, src, ACT.Copy, scale=1.0 if i < 2 else W3SHIFT).then_inc(wT_ready, 1)
                else:
                    dst = w2T[:, :, k * P:(k + 1) * P]
                    src = ps[0:HC, 4 + k, :].bitcast(F16)[:, 0:CH * P].rearrange("p (c n) -> p c n", c=CH)
                    nc.scalar.activation(dst, src, ACT.Copy).then_inc(wT_ready, 1)
            split_h2(NB - 1, 0)
            split_h2(NB - 1, 1)

            for gi in range(NG):
                for c in range(CH + 1):
                    n = gi * CH + c
                    if c < CH:
                        act.wait_ge(up_psum, n + 1)
                        if n == 0:
                            act.wait_ge(scale_ready, 2)
                        if n >= 2:
                            act.wait_ge(g_ready, n - 1)
                        nc.scalar.activation(u[:, n % 2, :], ps[0:HC, 2 * (n % 2), :], ACT.Tanh,
                                             scale=sgate[0:HC, :]).then_inc(tanh_done, 1)
                    if c >= 1:
                        m = n - 1
                        act.wait_ge(g_ready, m + 1)
                        if gi >= 1:
                            act.wait_ge(down_psum, 4 * gi)
                        nc.scalar.activation(gT[:, 0, c - 1, :], g[:, m % 2, :], ACT.Copy).then_inc(ghi, 1)

        @block.vector
        def _(dve):
            nc.vector.memset(w1n[96:HC, CH - 1, :], 0.0).then_inc(dve_pad, 1)
            nc.vector.memset(w3n[96:HC, CH - 1, :], 0.0).then_inc(dve_pad, 1)
            nc.vector.memset(w2n[:, :, HID:HP], 0.0).then_inc(dve_pad, 1)
            nc.vector.memset(wsum[:, :], 0.0).then_inc(dve_pad, 1)
            nc.vector.memset(scl[:, :], 0.0).then_inc(dve_pad, 1)
            steps = [0]

            def chain(ins):
                steps[0] += 1
                ins.then_inc(dve_step, 1)
                dve.wait_ge(dve_step, steps[0])

            def stats(src, st, mv, b, signal):
                for qt in range(2):
                    ins = nc.vector.bn_stats(st[:, 2 * b + qt, :], src[:, 2 * b + qt, :])
                    ins.then_inc(dve_step, 1)
                    steps[0] += 1
                dve.wait_ge(dve_step, steps[0])
                for qt in range(2):
                    last = nc.vector.bn_aggr(mv[:, 2 * b + qt, :], st[:, 2 * b + qt, :])
                    if qt == 0:
                        last.then_inc(dve_step, 1)
                        steps[0] += 1
                last.then_inc(signal, 1)

            def norm1(b):
                dve.wait_ge(rstd1, b + 1)
                for qt in range(2):
                    t = 2 * b + qt
                    nc.vector.tensor_scalar(hn[:, t, :], x_sb[:, t, :], mv1[:, t, 0:1], rs1[:, t, 1:2],
                                            ALU.subtract, ALU.mult).then_inc(normed1, 1)

            def rope(t):
                i, qt = t % 4, t % 2
                if t == 0:
                    dve.wait_ge(in_cst, 16)
                dve.wait_ge(qkv_psum, t + 1)
                qk = bank(6 + t % 2)[:, 0:NQK * HD].rearrange("p (h f e) -> p h f e", f=HD // 2, e=2)
                c = cos[:, qt].unsqueeze(1).broadcast_to([P, NQK, HD])
                s = sin[:, qt].rearrange("p (f e) -> p f e", e=2).unsqueeze(1).broadcast_to([P, NQK, HD // 2, 2])
                nc.vector.tensor_tensor(ra[:, i].rearrange("p (h d) -> p h d", d=HD),
                                        bank(6 + t % 2)[:, 0:NQK * HD].rearrange("p (h d) -> p h d", d=HD), c,
                                        ALU.mult)
                nc.vector.tensor_tensor(rb[:, i].rearrange("p (h f e) -> p h f e", f=HD // 2, e=2), qk[:, :, :, ::-1], s,
                                        ALU.mult).then_inc(rope_prod, 1)

            def evac_q(b, i):
                dve.wait_ge(stack_psum, 5 * b + i + 1)
                half, qt = i % 2, i // 2
                nc.vector.tensor_copy(qs[0:SLOT, b % 2, 8 * half:8 * half + 8, qt * P:(qt + 1) * P],
                                      ps[0:SLOT, i, :].bitcast(BF16).rearrange("p (h n) -> p h n", n=P)
                                      ).then_inc(stack_dve, 1)

            def evac_k(b):
                dve.wait_ge(stack_psum, 5 * b + 5)
                nc.vector.tensor_copy(ks[0:SLOT, b % 2, :, :].rearrange("p k s -> p (k s)"),
                                      ps[0:SLOT, 7, :].bitcast(BF16)).then_inc(stack_dve, 1)

            def row_max(b, w):
                qt, kv, rp = w // 8, (w // 2) % 4, w % 2
                dve.wait_ge(max_psum, 16 * b + w + 1)
                if w == 0 and b >= 1:
                    dve.wait_ge(nms_ready, b)
                nc.vector.tensor_reduce(nmx[:, qt, 2 * rp * NKV + kv:(2 * rp + 1) * NKV + kv + 1:NKV],
                                        bank(4 + w % 2).rearrange("p (r s) -> p r s", r=2),
                                        axis=AX.X, op=ALU.max, negate=True).then_inc(max_done, 1)

            def split_max(b):
                dve.wait_ge(max_done, 16 * b + 16)
                if b >= 1:
                    dve.wait_ge(nmT_psum, b)
                chain(nc.vector.tensor_copy(nms[:, :, 0, :], nmx[:, :, :]))
                chain(nc.vector.tensor_tensor(nmr[:, :, :], nmx[:, :, :], nms[:, :, 0, :], ALU.subtract))
                chain(nc.vector.tensor_copy(nms[:, :, 1, :], nmr[:, :, :]))
                nc.vector.tensor_tensor(nms[:, :, 2, :], nmr[:, :, :], nms[:, :, 1, :],
                                        ALU.subtract).then_inc(nms_ready, 1)

            def evac_max(b):
                dve.wait_ge(nmT_psum, b + 1)
                if b >= 2:
                    dve.wait_ge(mrows, 16 * MROW * (b - 1))
                nc.vector.tensor_copy(nmT[:, b % 2, :], ps[0:MROW * NH, 5, 0:S // 2].bitcast(BF16)).then_inc(nmT_ready, 1)

            def normalise(b, qt):
                dve.wait_ge(o_psum, 2 * b + qt + 1)
                if b >= 1:
                    dve.wait_ge(oT_psum, 2 * b - 1 + qt)
                o = bank(qt).rearrange("p (k r c) -> p k r c", k=NKV, r=REP)
                rd = rden[:, qt].rearrange("p (k r) -> p k r", k=NKV)
                chain(nc.vector.reciprocal(rd, o[:, :, :, HD]))
                nc.vector.tensor_tensor(on[:, qt].rearrange("p r k d -> p k r d"), o[:, :, :, 0:HD],
                                        rd.unsqueeze(3).broadcast_to([P, NKV, REP, HD]),
                                        ALU.mult).then_inc(on_ready, 1)

            def residual(b, qt):
                t = 2 * b + qt
                dve.wait_ge(wo_psum, t + 1)
                nc.vector.tensor_tensor(x1[:, t, :], x_sb[:, t, :], bank(4 + qt, D), ALU.add).then_inc(x1_ready, 1)

            def norm2(b):
                dve.wait_ge(rstd2, b + 1)
                for qt in range(2):
                    t = 2 * b + qt
                    if b >= 1:
                        dve.wait_ge(h2T_psum, t - 1)
                    nc.vector.tensor_scalar(h2[:, qt, :], x1[:, t, :], mv2[:, t, 0:1], rs2[:, t, 1:2],
                                            ALU.subtract, ALU.mult).then_inc(h2_ready, 1)

            def split_h2(b, qt):
                t = 2 * b + qt
                dve.wait_ge(h2hi, t + 1)
                sl = slice(t * P, (t + 1) * P)
                nc.vector.tensor_tensor(h2T[:, 1, :, sl], bank(7, D).rearrange("p (k n) -> p k n", k=KC),
                                        h2T[:, 0, :, sl], ALU.subtract).then_inc(h2lo, 1)

            def layer_norm2_stats(b):
                dve.wait_ge(x1_ready, 2 * b + 2)
                stats(x1, st2, mv2, b, var2)

            for b in range(2):
                dve.wait_ge(in_x[b], 16)
                stats(x_sb, st1, mv1, b, var1)
                norm1(b)
            rope(0)
            rope(1)
            for b in range(2, NB):
                dve.wait_ge(in_x[b], 16)
                stats(x_sb, st1, mv1, b, var1)
            evac_q(0, 1)
            evac_q(0, 3)
            evac_k(0)
            rope(2)
            rope(3)
            norm1(2)
            norm1(3)
            for w in range(16):
                row_max(0, w)
                if w == 9:
                    evac_q(1, 1)
                    evac_q(1, 3)
                    evac_k(1)
            split_max(0)
            evac_max(0)

            for b in range(NB):
                t = 2 * b + 4
                if b >= 1:
                    normalise(b - 1, 0)
                    normalise(b - 1, 1)
                if t < NT:
                    rope(t)
                    rope(t + 1)
                if b >= 1:
                    residual(b - 1, 0)
                    residual(b - 1, 1)
                    layer_norm2_stats(b - 1)
                for v in range(8):
                    if b + 1 < NB:
                        row_max(b + 1, 2 * v)
                        row_max(b + 1, 2 * v + 1)
                    if b >= 1 and v == 0:
                        norm2(b - 1)
                    if b >= 1 and v == 6:
                        split_h2(b - 1, 0)
                    if b >= 1 and v == 7:
                        split_h2(b - 1, 1)
                if b + 1 < NB:
                    split_max(b + 1)
                if b + 2 < NB:
                    evac_q(b + 2, 1)
                    evac_q(b + 2, 3)
                    evac_k(b + 2)
                if b + 1 < NB:
                    evac_max(b + 1)
                if b == NB - 1:
                    dve.wait_ge(wtot_psum, 1)
                    chain(nc.vector.tensor_scalar(scl[:, :], bank(4, 3), 1.0 / (HID * D), None, ALU.mult))
                    nc.vector.tensor_scalar(thr[:, :], scl[:, :], 0.5, None, ALU.mult)
                    nc.vector.tensor_scalar(nthr[:, :], scl[:, :], -0.5, None, ALU.mult)
                    nc.vector.tensor_scalar(sgate[:, :], scl[:, 0:1], -0.5, None, ALU.mult).then_inc(scale_ready, 1)
                    chain(nc.vector.tensor_tensor(sout[:, 0:1], scl[:, 0:1], scl[:, 1:2], ALU.mult))
                    nc.vector.scalar_tensor_tensor(sout[:, 1:2], sout[:, 0:1], -0.5 / W3SHIFT, scl[:, 2:3],
                                                   ALU.mult, ALU.mult).then_inc(scale_ready, 1)
                    for i, wn in enumerate((w1n, w3n, w2n)):
                        n = HC if i < 2 else P
                        src = wn[:, :, :].rearrange("p c d -> p (c d)")
                        m = src.shape[1]
                        chain(nc.vector.tensor_scalar(tpos[0:n, 0:m], src, thr[0:n, i:i + 1], None, ALU.is_gt))
                        nc.vector.scalar_tensor_tensor(tern[0:n, i, 0:m], src, nthr[0:n, i:i + 1], tpos[0:n, 0:m],
                                                       ALU.is_lt, ALU.subtract).then_inc(tern_ready, 1)
                        dve.wait_ge(tern_ready, i + 1)
            b = NB - 1
            normalise(b, 0)
            normalise(b, 1)
            residual(b, 0)
            residual(b, 1)
            layer_norm2_stats(b)
            norm2(b)
            split_h2(b, 0)
            split_h2(b, 1)

            def gate(n):
                yb = 2 * (n % 2)
                dve.wait_ge(tanh_done, n + 1)
                if n >= 2:
                    dve.wait_ge(glo, n - 1)
                chain(nc.vector.scalar_tensor_tensor(uv[:, n % 2, :], u[:, n % 2, :], 1.0, ps[0:HC, yb, :],
                                                     ALU.add, ALU.mult))
                nc.vector.tensor_tensor(g[:, n % 2, :], uv[:, n % 2, :], ps[0:HC, yb + 1, :],
                                        ALU.mult).then_inc(g_ready, 1)

            def gate_lo(n):
                gi, c = n // CH, n % CH
                dve.wait_ge(ghi, n + 1)
                nc.vector.tensor_tensor(gT[:, 1, c, :], g[:, n % 2, :], gT[:, 0, c, :],
                                        ALU.subtract).then_inc(glo, 1)

            for gi in range(NG):
                for c in range(CH + 1):
                    n = gi * CH + c
                    if c < CH:
                        gate(n)
                    if c >= 1:
                        gate_lo(n - 1)
                for j in range(GT // P):
                    t = gi * (GT // P) + j
                    dve.wait_ge(down_psum, t + 1)
                    if t >= 2:
                        dve.wait_ge(stored[t % 2], 16 * (t // 2))
                    nc.vector.scalar_tensor_tensor(y[:, t % 2, :], bank(6 + t % 2, D), sout[:, 1:2], x1[:, t, :],
                                                   ALU.mult, ALU.add).then_inc(y_ready, 1)

        @block.tensor
        def _(pe):
            def tr_h(t):
                pe.wait_ge(normed1, t + 1)
                if t == 0:
                    pe.wait_ge(in_cst, 16)
                if t >= 2:
                    pe.wait_ge(hT_ready, t - 1)
                for k in range(KC):
                    last = nc.tensor.transpose(bank(2 + t % 2)[:, k * P:(k + 1) * P], hn[:, t, k * P:(k + 1) * P], id32)
                last.then_inc(hT_psum, 1)

            def project(t):
                pe.wait_ge(hT_ready, t + 1)
                if t == 0:
                    pe.wait_ge(in_wqkv, 48)
                if t >= 2:
                    pe.wait_ge(v_ready, t - 1)
                if t >= 3 and t % 2:
                    pe.wait_ge(stack_dve, 3 * (t - 1) // 2)
                for k in range(KC):
                    last = nc.tensor.matmul(bank(6 + t % 2, QKV), hT[:, t % 2, k, :], wqkv_sb[:, k, :],
                                            start=(k == 0), stop=(k == KC - 1))
                last.then_inc(qkv_psum, 1)

            def stack_q(b, i):
                half, qt = i % 2, i // 2
                t = 2 * b + qt
                pe.wait_ge(parts_ready, 2 * t + 2)
                if t == 0:
                    pe.wait_ge(idents, 1)
                dst = ps[0:SLOT, i, :].bitcast(BF16)
                for j in range(8):
                    last = nc.tensor.transpose(dst[:, j * P:(j + 1) * P],
                                               part[:, t % 4, 8 * half + j].rearrange("p s d -> p (s d)"), idb[:, :])
                last.then_inc(stack_psum, 1)

            def stack_k(b):
                dst = ps[0:SLOT, 7, :].bitcast(BF16)
                for kv in range(NKV):
                    for kt in range(2):
                        j = 2 * kv + kt
                        last = nc.tensor.transpose(dst[:, j * P:(j + 1) * P],
                                                   part[:, (2 * b + kt) % 4, NH + kv].rearrange("p s d -> p (s d)"), idb[:, :])
                last.then_inc(stack_psum, 1)

            def max_scores(b, w):
                qt, kv, rp = w // 8, (w // 2) % 4, w % 2
                n = 16 * b + w
                if w == 0:
                    pe.wait_ge(stack_act, 2 * b + 2)
                    pe.wait_ge(stack_dve, 3 * b + 3)
                if w == 0 and b >= 1:
                    pe.wait_ge(nmT_ready, b)
                if w == 0 and b >= 2:
                    pe.wait_ge(x1_ready, 2 * (b - 1))
                if n >= 2:
                    pe.wait_ge(max_done, n - 1)
                for r in range(2):
                    last = nc.tensor.matmul(bank(4 + w % 2)[:, r * S:(r + 1) * S],
                                            qs[0:SLOT, b % 2, (2 * rp + r) * NKV + kv, qt * P:(qt + 1) * P],
                                            ks[0:SLOT, b % 2, kv, :], start=True, stop=True)
                last.then_inc(max_psum, 1)

            def scores(b, v):
                n, kv, kt = 8 * b + v, v // 2, v % 2
                if v == 0:
                    pe.wait_ge(mrows, 16 * MROW * (b + 1))
                    pe.wait_ge(pool_init, 4)
                if v == 0:
                    pe.wait_ge(stack_act, 2 * min(b + 2, NB))
                    pe.wait_ge(stack_dve, 3 * min(b + 2, NB) - 1)
                    pe.wait_ge(hT_ready, min(2 * b + 6, NT))
                    if b >= 1:
                        pe.wait_ge(on_ready, 2 * b)
                if n >= 2:
                    pe.wait_ge(exp_done, n - 1)
                for h in range(2):
                    last = nc.tensor.matmul(bank(2 * (n % 2) + h), ks[0:SLOT + MROW, b % 2, kv, kt * P:(kt + 1) * P],
                                            qs[0:SLOT + MROW, b % 2, 2 * h * NKV + kv:(2 * h + 1) * NKV + kv + 1:NKV, :],
                                            start=True, stop=True)
                last.then_inc(score_psum, 1)

            def pv(b, v):
                n, kv, kt = 8 * b + v, v // 2, v % 2
                pe.wait_ge(exp_done, n + 1)
                if v == 0:
                    pe.wait_ge(v_ready, min(2 * b + 5, NT))
                    if b >= 1:
                        pe.wait_ge(ot_ready, 2 * b)
                if v == 4:
                    pe.wait_ge(ot_ready, 2 * b + 1)
                for r in range(REP):
                    last = nc.tensor.matmul(ps[VW * r:VW * (r + 1), 6, (kv % 2) * S:(kv % 2 + 1) * S],
                                            vst[:, 2 * b + kt, kv, :], pt[:, n % 3, r, :],
                                            start=(kt == 0), stop=(kt == 1))
                last.then_inc(pv_done, 1)

            def tr_max(b):
                pe.wait_ge(nms_ready, b + 1)
                dst = ps[0:MROW * NH, 5, 0:S // 2].bitcast(BF16)
                for qt in range(2):
                    last = nc.tensor.transpose(dst[:, qt * P:(qt + 1) * P], nms[:, qt].rearrange("p m h -> p (m h)"), idb[:, :])
                last.then_inc(nmT_psum, 1)

            def tr_o(b, qt):
                if qt == 0:
                    pe.wait_ge(ot_ready, 2 * b + 2)
                    pe.wait_ge(stack_act, 2 * min(b + 3, NB))
                    pe.wait_ge(stack_dve, 3 * min(b + 3, NB) - 1)
                for kv in range(NKV):
                    last = nc.tensor.transpose(bank(qt)[:, kv * P:(kv + 1) * P], ot[:, kv, qt * P:(qt + 1) * P], id32)
                last.then_inc(o_psum, 1)

            def tr_on(b, qt):
                pe.wait_ge(on_ready, 2 * b + qt + 1)
                if b + 1 < NB:
                    pe.wait_ge(max_done, 16 * (b + 2))
                    pe.wait_ge(nmT_ready, b + 2)
                o = on[:, qt].rearrange("p r k d -> p (r k d)")
                for k in range(KC):
                    last = nc.tensor.transpose(bank(4 + qt)[:, k * P:(k + 1) * P], o[:, k * P:(k + 1) * P], id32)
                last.then_inc(oT_psum, 1)

            def out_proj(b, qt):
                pe.wait_ge(oT_ready, 2 * b + qt + 1)
                if b == 0 and qt == 0:
                    pe.wait_ge(in_wo, 16)
                for k in range(KC):
                    last = nc.tensor.matmul(bank(4 + qt, D), oT[:, qt, k, :], wo_sb[:, k, :],
                                            start=(k == 0), stop=(k == KC - 1))
                last.then_inc(wo_psum, 1)

            def tr_h2(b, qt):
                pe.wait_ge(h2_ready, 2 * b + qt + 1)
                for k in range(KC):
                    last = nc.tensor.transpose(bank(7)[:, k * P:(k + 1) * P], h2[:, qt, k * P:(k + 1) * P], id32)
                last.then_inc(h2T_psum, 1)

            tr_h(0)
            tr_h(1)
            project(0)
            project(1)
            tr_h(2)
            tr_h(3)
            stack_q(0, 0)
            stack_q(0, 1)
            pe.wait_ge(hT_ready, 4)
            stack_q(0, 2)
            stack_q(0, 3)
            pe.wait_ge(v_ready, 2)
            stack_k(0)
            project(2)
            project(3)
            for w in range(16):
                max_scores(0, w)
                if w == 7:
                    for i in range(4):
                        stack_q(1, i)
                    pe.wait_ge(v_ready, 4)
                    stack_k(1)
            tr_max(0)

            for b in range(NB):
                t = 2 * b + 4
                if b >= 1:
                    tr_o(b - 1, 0)
                    tr_o(b - 1, 1)
                if t < NT:
                    pe.wait_ge(stack_act, 2 * (b + 2))
                    pe.wait_ge(stack_dve, 3 * (b + 2) - 1)
                    tr_h(t)
                    tr_h(t + 1)
                if b >= 1:
                    tr_on(b - 1, 0)
                    tr_on(b - 1, 1)
                if t < NT:
                    if b >= 1:
                        pe.wait_ge(ot_ready, 2 * b)
                    project(t)
                    project(t + 1)
                if b >= 1:
                    out_proj(b - 1, 0)
                    out_proj(b - 1, 1)
                for v in range(8):
                    scores(b, v)
                    if b + 1 < NB:
                        max_scores(b + 1, 2 * v)
                        max_scores(b + 1, 2 * v + 1)
                    if v >= 1:
                        pv(b, v - 1)
                    if b >= 1 and v == 3:
                        pe.wait_ge(v_ready, min(2 * b + 6, NT))
                        pe.wait_ge(stack_dve, 3 * min(b + 2, NB))
                        if b >= 2:
                            pe.wait_ge(h2lo, 2 * b - 2)
                        tr_h2(b - 1, 0)
                    if b >= 1 and v == 6:
                        pe.wait_ge(h2lo, 2 * b - 1)
                        tr_h2(b - 1, 1)
                pv(b, 7)
                if b + 2 < NB:
                    pe.wait_ge(exp_done, 8 * b + 8)
                    for i in range(4):
                        stack_q(b + 2, i)
                    if b >= 1:
                        pe.wait_ge(h2lo, 2 * b)
                    else:
                        pe.wait_ge(v_ready, 6)
                    stack_k(b + 2)
                if b + 1 < NB:
                    tr_max(b + 1)
                if b == NB - 1:
                    pe.wait_ge(wsum_ready, 1)
                    pe.wait_ge(pool_init, 5)
                    pe.wait_ge(x1_ready, 2 * b)
                    nc.tensor.matmul(bank(4, 3), ones[:, :], wsum[:, :], start=True, stop=True).then_inc(wtot_psum, 1)
            b = NB - 1
            tr_o(b, 0)
            tr_o(b, 1)
            tr_on(b, 0)
            tr_on(b, 1)
            out_proj(b, 0)
            out_proj(b, 1)
            pe.wait_ge(x1_ready, 2 * NB)
            pe.wait_ge(idents, 2)
            for i in range(6):
                k, w = i % 2, i // 2
                pe.wait_ge(tern_ready, w + 1)
                if i >= 2:
                    pe.wait_ge(wT_ready, i - 1)
                for c in range(CH):
                    if w < 2:
                        src = tern[0:HC, w, c * D + k * P:c * D + (k + 1) * P]
                        last = nc.tensor.transpose(bank(4 + k).bitcast(F16)[:, c * HC:(c + 1) * HC], src, idh[0:HC, 0:HC])
                    else:
                        src = tern[:, 2, k * HP + c * HC:k * HP + (c + 1) * HC]
                        last = nc.tensor.transpose(ps[0:HC, 4 + k, :].bitcast(F16)[:, c * P:(c + 1) * P], src, idh[:, :])
                last.then_inc(wT_psum, 1)
            pe.wait_ge(h2lo, 2 * NB - 2)
            tr_h2(b, 0)
            pe.wait_ge(h2lo, 2 * NB - 1)
            tr_h2(b, 1)

            def up(n):
                gi, c = n // CH, n % CH
                yb = 2 * (n % 2)
                if c == 0:
                    pe.wait_ge(h2lo, (gi + 1) * (GT // P))
                if n == 0:
                    pe.wait_ge(wT_ready, 4)
                    pe.wait_ge(on_ready, 2 * NB)
                if n >= 2:
                    pe.wait_ge(g_ready, n - 1)
                for m, wT in enumerate((w1T, w3T)):
                    for i in range(2 * KC):
                        k, part_ = i // 2, i % 2
                        last = nc.tensor.matmul(ps[0:HC, yb + m, :], wT[:, k, c * HC:(c + 1) * HC],
                                                h2T[:, part_, k, gi * GT:(gi + 1) * GT],
                                                start=(i == 0), stop=(i == 2 * KC - 1))
                last.then_inc(up_psum, 1)

            def down(gi, j):
                t = gi * (GT // P) + j
                if j == 0:
                    pe.wait_ge(glo, CH * (gi + 1))
                if t == 0:
                    pe.wait_ge(wT_ready, 6)
                    pe.wait_ge(h2lo, 2 * NB)
                if t >= 2:
                    pe.wait_ge(y_ready, t - 1)
                for c in range(CH):
                    for h in range(2):
                        last = nc.tensor.matmul(bank(6 + t % 2, D), gT[:, h, c, j * P:(j + 1) * P], w2T[:, c, :],
                                                start=(c == 0 and h == 0), stop=(c == CH - 1 and h == 1))
                last.then_inc(down_psum, 1)

            for gi in range(NG):
                for c in range(CH):
                    up(gi * CH + c)
                for j in range(GT // P):
                    down(gi, j)


_W = ("L0_attn_W_q", "L0_attn_W_k", "L0_attn_W_v", "L0_attn_W_o", "L0_ffn_w1", "L0_ffn_w3", "L0_ffn_w2")


def _constants():
    half = HD // 2
    freq = (np.float32(1.0) / np.float32(10000.0) ** (np.arange(half, dtype=np.float32) / np.float32(half))).astype(np.float32)
    ang = np.arange(S, dtype=np.float32)[:, None] * freq[None, :]
    c, s = np.cos(ang).astype(np.float32), np.sin(ang).astype(np.float32)
    cos = np.repeat(c, 2, axis=1)
    sin = np.stack([-s, s], axis=-1).reshape(S, HD)
    tiles = [a.reshape(2, P, HD).transpose(1, 0, 2).reshape(P, 2 * HD) for a in (cos, sin)]
    return np.ascontiguousarray(np.concatenate([np.eye(P, dtype=np.float32), *tiles], axis=1))


def kernel(**inputs):
    import concourse.bacc as bacc
    from concourse.bass_utils import run_bass_kernel_spmd

    nc = bacc.Bacc("TRN2", target_bir_lowering=False, num_devices=1)
    arrays = {"x": np.ascontiguousarray(inputs["L0_attn_x"]), "consts": _constants()}
    for name in _W:
        arrays[name] = np.ascontiguousarray(inputs[name])
    aps = {n: nc.dram_tensor(n, a.shape, mybir.dt.from_np(a.dtype), kind="ExternalInput").ap() for n, a in arrays.items()}
    out = nc.dram_tensor("out", (NB, S, D), F32, kind="ExternalOutput").ap()
    w = [aps[n] for n in _W]
    build(nc, aps["x"], w[0:3], w[3], w[4], w[5], w[6], aps["consts"], out)
    r = run_bass_kernel_spmd(nc, [arrays], core_ids=[0])
    return r.results[0]["out"]
```

```python
from contextlib import ExitStack

import numpy as np

import concourse.bass as bass
from concourse import mybir

F32 = mybir.dt.float32
BF16 = mybir.dt.bfloat16
F16 = mybir.dt.float16
ALU = mybir.AluOpType
ACT = mybir.ActivationFunctionType
AX = mybir.AxisListType

P = 128
NB, S, D = 4, 256, 256
NT = NB * S // P
HD, NKV, REP = 16, 4, 4
NH = NKV * REP
NQK = NH + NKV
QKV = D + 2 * NKV * HD
KC = D // P
HID = int(2 * D * 4 / 3)
CH = 6
HC = 114
HP = CH * HC
LAST = HID - (CH - 1) * HC
SLOT = 6 * HD
MROW = 3
EPS = 1e-5
UPS = (1, 2, 1, 2, 1, 2, 1, 2)
NU = NB * CH
W3SHIFT = 2.0 ** -6
VW = 32


def build(nc, x, wqkv, wo, w1, w3, w2, consts, out):
    ctx = ExitStack()
    with ctx:
        def sb(name, shape, dt=F32):
            return ctx.enter_context(nc.sbuf_tensor(name, shape, dt))

        def sem(name):
            return ctx.enter_context(nc.semaphore(name))

        x_sb = sb("x_sb", [P, NT, D])
        x1 = sb("x1", [P, NT, D])
        wqkv_sb = sb("wqkv_sb", [P, KC, QKV])
        wo_sb = sb("wo_sb", [P, KC, D])
        cst = sb("cst", [P, P + 4 * HD])
        id32 = cst[:, 0:P]
        cos = cst[:, P:P + 2 * HD].rearrange("p (q d) -> p q d", q=2)
        sin = cst[:, P + 2 * HD:P + 4 * HD].rearrange("p (q d) -> p q d", q=2)
        idb = sb("idb", [P, P], BF16)
        idh = sb("idh", [P, P], F16)
        ones = sb("ones", [P, P])
        mhalf = sb("mhalf", [P, 2])
        st1 = sb("st1", [P, NT, 6])
        mv1 = sb("mv1", [P, NT, 2])
        rs1 = sb("rs1", [P, NT, 2])
        hn = sb("hn", [P, NT, D])
        hT = sb("hT", [P, 2, KC, P])
        ra = sb("ra", [P, 4, NQK * HD])
        rb = sb("rb", [P, 4, NQK * HD])
        rq = sb("rq", [P, 4, NQK * HD])
        r1 = sb("r1", [P, 4, NQK * HD])
        part = sb("part", [P, 4, NQK, 6, HD], BF16)
        vst = sb("vst", [P, NT, NKV, VW])
        qs = sb("qs", [P, 2, NH, S], BF16)
        ks = sb("ks", [P, 2, NKV, S], BF16)
        nmx = sb("nmx", [P, 2, NH])
        nmr = sb("nmr", [P, 2, NH])
        nms = sb("nms", [P, 2, MROW, NH], BF16)
        nmT = sb("nmT", [MROW * NH, 2, S], BF16)
        pt = sb("pt", [P, 3, REP, S])
        ot = sb("ot", [P, NKV, S])
        rden = sb("rden", [P, 2, NH])
        on = sb("on", [P, 2, REP, NKV, HD])
        oT = sb("oT", [P, 2, KC, P])
        st2 = sb("st2", [P, NT, 6])
        mv2 = sb("mv2", [P, NT, 2])
        rs2 = sb("rs2", [P, NT, 2])
        h2 = sb("h2", [P, 2, D])
        h2T = sb("h2T", [P, 2, KC, NB * S], F16)
        w1n = sb("w1n", [HC, CH, D])
        w3n = sb("w3n", [HC, CH, D])
        w2n = sb("w2n", [P, KC, HP])
        tern = sb("tern", [P, 3, CH * D], F16)
        tpos = sb("tpos", [P, CH * D], F16)
        tneg = sb("tneg", [P, CH * D], F16)
        wabs = sb("wabs", [P, CH * D], BF16)
        wsum = sb("wsum", [P, 3])
        scl = sb("scl", [P, 3])
        thr = sb("thr", [P, 3])
        nthr = sb("nthr", [P, 3])
        sgate = sb("sgate", [P, 1])
        sout = sb("sout", [P, 2])
        w1T = sb("w1T", [P, KC, HP], F16)
        w3T = sb("w3T", [P, KC, HP], F16)
        w2T = sb("w2T", [HC, CH, D], F16)
        u = sb("u", [HC, 3, S])
        uv = sb("uv", [HC, 3, S])
        g = sb("g", [HC, 3, S])
        gT = sb("gT", [HC, 2, NU, S], F16)
        y = hn

        ps = ctx.enter_context(nc.psum_tensor("ps", [P, 8, 512], F32))

        def bank(i, n=512):
            return ps[:, i, 0:n]

        in_x = [sem(f"in_x{b}") for b in range(NB)]
        in_cst, in_wqkv, in_wo = sem("in_cst"), sem("in_wqkv"), sem("in_wo")
        in_w = [sem(f"in_w{i}") for i in range(3)]
        pool_init, dve_pad, idents = sem("pool_init"), sem("dve_pad"), sem("idents")
        dve_step, pool_step = sem("dve_step"), sem("pool_step")
        var1, rstd1, normed1 = sem("var1"), sem("rstd1"), sem("normed1")
        hT_psum, hT_ready, qkv_psum = sem("hT_psum"), sem("hT_ready"), sem("qkv_psum")
        rope_prod, v_ready, roped = sem("rope_prod"), sem("v_ready"), sem("roped")
        p0k_ready, p1k_ready = sem("p0k_ready"), sem("p1k_ready")
        p0_ready, r1_ready, p1_ready, parts_ready = sem("p0_ready"), sem("r1_ready"), sem("p1_ready"), sem("parts_ready")
        stack_psum, stack_act, stack_dve = sem("stack_psum"), sem("stack_act"), sem("stack_dve")
        max_psum, max_done, nms_ready = sem("max_psum"), sem("max_done"), sem("nms_ready")
        nmT_psum, nmT_ready, mrows = sem("nmT_psum"), sem("nmT_ready"), sem("mrows")
        score_psum, exp_done, pv_done = sem("score_psum"), sem("exp_done"), sem("pv_done")
        ot_ready, o_psum, on_ready = sem("ot_ready"), sem("o_psum"), sem("on_ready")
        oT_psum, oT_ready, wo_psum, x1_ready = sem("oT_psum"), sem("oT_ready"), sem("wo_psum"), sem("x1_ready")
        var2, rstd2, h2_ready, h2T_psum = sem("var2"), sem("rstd2"), sem("h2_ready"), sem("h2T_psum")
        h2hi, h2lo = sem("h2hi"), sem("h2lo")
        wsum_ready, wtot_psum, scale_ready, tern_ready = sem("wsum_ready"), sem("wtot_psum"), sem("scale_ready"), sem("tern_ready")
        wT_psum, wT_act, wT_dve = sem("wT_psum"), sem("wT_act"), sem("wT_dve")
        up_psum, tanh_done, g_ready, ghi, glo = sem("up_psum"), sem("tanh_done"), sem("g_ready"), sem("ghi"), sem("glo")
        down_psum, y_ready, stored = sem("down_psum"), sem("y_ready"), sem("stored")

        def proj_bank(b, qt):
            return bank((6, 3)[qt] if b == NB - 1 else 4 + qt, D)

        def up_bank(n):
            return 4 + n % 2 if n < NU - CH else (4, 5, 1)[n % 3]

        def down_bank(t):
            return bank((7, 2, 7)[t // 2])[:, (t % 2) * D:(t % 2 + 1) * D] if t < NT - 2 else bank((2, 3)[t % 2], D)

        def h2_bank(b, qt):
            return bank(qt if b == NB - 1 else 7, D).rearrange("p (k n) -> p k n", k=KC)

        def first_unit(v):
            return sum(UPS[:v])

        block = ctx.enter_context(nc.Block())

        @block.sync
        def _(sp):
            def load_x(b):
                sp.dma_start(x_sb[:, 2 * b:2 * b + 2, :],
                             x[b].rearrange("(t p) d -> p t d", p=P)).then_inc(in_x[b], 16)

            load_x(0)
            sp.dma_start(cst[:, :], consts).then_inc(in_cst, 16)
            for i, w in enumerate(wqkv):
                n0 = (0, D, D + NKV * HD)[i]
                sp.dma_start(wqkv_sb[:, :, n0:n0 + w.shape[1]],
                             w.rearrange("(k p) n -> p k n", p=P)).then_inc(in_wqkv, 16)
            for b in range(1, NB):
                load_x(b)
            sp.dma_start(wo_sb[:, :, :], wo.rearrange("(k p) n -> p k n", p=P)).then_inc(in_wo, 16)
            sp.wait_ge(dve_pad, 3)
            for i, (w, wn) in enumerate(((w1, w1n), (w3, w3n))):
                sp.dma_start(wn[:, 0:CH - 1, :],
                             w[0:(CH - 1) * HC, :].rearrange("(c p) d -> p c d", p=HC)).then_inc(in_w[i], 16)
                sp.dma_start(wn[0:LAST, CH - 1, :], w[(CH - 1) * HC:HID, :]).then_inc(in_w[i], 16)
            sp.dma_start(w2n[:, :, 0:HID], w2.rearrange("(k p) h -> p k h", p=P)).then_inc(in_w[2], 16)

            def max_rows(b):
                sp.wait_ge(nmT_ready, b + 1)
                for m in range(MROW):
                    sp.dma_start(qs[SLOT + m:SLOT + m + 1, b % 2, :, :],
                                 nmT[m * NH:(m + 1) * NH, b % 2, :]).then_inc(mrows, 16)

            for b in range(NB):
                max_rows(b)
            for b in range(NB - 1):
                sp.wait_ge(y_ready, b + 1)
                sp.dma_start(out[b].rearrange("(t p) d -> p t d", p=P), y[:, 2 * b:2 * b + 2, :]).then_inc(stored, 16)
            for qt in range(2):
                sp.wait_ge(y_ready, NB + qt)
                sp.dma_start(out[NB - 1, qt * P:(qt + 1) * P, :], y[:, NT - 2 + qt, :]).then_inc(stored, 16)
            sp.wait_ge(stored, 16 * (NB + 1))

        @block.gpsimd
        def _(pool):
            for n, (dst, value) in enumerate(((mhalf[:, :], -0.5), (vst[:, :, :, :], 0.0),
                                              (vst[:, :, :, HD:HD + 1], 1.0),
                                              (ks[SLOT:SLOT + MROW, :, :, :], 1.0), (ones[:, :], 1.0))):
                nc.gpsimd.memset(dst, value).then_inc(pool_init, 1)
                pool.wait_ge(pool_init, n + 1)
            steps = [0]

            def chain(ins):
                steps[0] += 1
                ins.then_inc(pool_step, 1)
                pool.wait_ge(pool_step, steps[0])

            def rsqrt(rs, var, b):
                sl = slice(2 * b, 2 * b + 2)
                chain(nc.gpsimd.tensor_scalar(rs[:, sl, 0], var[:, sl, 1], EPS, None, ALU.add))
                return nc.gpsimd.tensor_tensor(rs[:, sl, 1], rs[:, sl, 0], mhalf[:, :], ALU.pow)

            def rsqrt1(b):
                pool.wait_ge(var1, b + 1)
                rsqrt(rs1, mv1, b).then_inc(rstd1, 1)

            def rsqrt2(b):
                pool.wait_ge(var2, b + 1)
                rsqrt(rs2, mv2, b).then_inc(rstd2, 1)

            def split(t):
                i = t % 4
                q, k = part[:, i, 0:NH], part[:, i, NH:NQK]
                heads = lambda a: a[:, i].rearrange("p (h d) -> p h d", d=HD)
                pool.wait_ge(rope_prod, t + 1)
                nc.gpsimd.tensor_tensor(rq[:, i], ra[:, i], rb[:, i], ALU.add).then_inc(roped, 1)
                pool.wait_ge(roped, t + 1)
                nc.gpsimd.tensor_copy(k[:, :, 1:6:2, :], heads(rq)[:, NH:NQK].unsqueeze(2).broadcast_to([P, NKV, 3, HD])
                                      ).then_inc(p0k_ready, 1)
                pool.wait_ge(p0k_ready, t + 1)
                pool.wait_ge(p0_ready, t + 1)
                nc.gpsimd.tensor_tensor(heads(r1), heads(rq), part[:, i, :, 1, :], ALU.subtract).then_inc(r1_ready, 1)
                pool.wait_ge(r1_ready, t + 1)
                nc.gpsimd.tensor_copy(k[:, :, 0:5:4, :], heads(r1)[:, NH:NQK].unsqueeze(2).broadcast_to([P, NKV, 2, HD])
                                      ).then_inc(p1k_ready, 1)
                pool.wait_ge(p1k_ready, t + 1)
                nc.gpsimd.tensor_tensor(k[:, :, 2, :], heads(r1)[:, NH:NQK], k[:, :, 4, :], ALU.subtract
                                        ).then_inc(parts_ready, 1)
                pool.wait_ge(p1_ready, t + 1)
                nc.gpsimd.tensor_tensor(q[:, :, 5, :], heads(r1)[:, 0:NH], q[:, :, 4, :], ALU.subtract
                                        ).then_inc(parts_ready, 1)

            def ternary(i):
                if i == 0:
                    pool.wait_ge(scale_ready, 3)
                n, m = (HC, CH * D) if i < 2 else (P, KC * HP)
                src = (w1n, w3n, w2n)[i][:, :, :].rearrange("p c d -> p (c d)")
                chain(nc.gpsimd.tensor_scalar(tpos[0:n, 0:m], src, thr[0:n, i:i + 1], None, ALU.is_gt))
                chain(nc.gpsimd.tensor_scalar(tneg[0:n, 0:m], src, nthr[0:n, i:i + 1], None, ALU.is_lt))
                nc.gpsimd.tensor_tensor(tern[0:n, i, 0:m], tneg[0:n, 0:m], tpos[0:n, 0:m],
                                        ALU.subtract).then_inc(tern_ready, 1)
                pool.wait_ge(tern_ready, i + 1)

            def gate_lo(n):
                pool.wait_ge(ghi, n + 1)
                nc.gpsimd.tensor_tensor(gT[:, 1, n, :], g[:, n % 3, :], gT[:, 0, n, :],
                                        ALU.subtract).then_inc(glo, 1)

            rsqrt1(0)
            rsqrt1(1)
            split(0)
            split(1)
            rsqrt1(2)
            rsqrt1(3)
            split(2)
            split(3)
            for b in range(NB):
                if b >= 1:
                    rsqrt2(b - 1)
                if b + 2 < NB:
                    split(2 * b + 4)
                    split(2 * b + 5)
                if b < 3:
                    ternary(b)
            for n in range(NU):
                if n == 2 * CH + 3:
                    rsqrt2(NB - 1)
                gate_lo(n)

        @block.scalar
        def _(act):
            act.wait_ge(in_cst, 16)
            nc.scalar.activation(idb[:, :], id32, ACT.Copy).then_inc(idents, 1)
            nc.scalar.activation(idh[:, :], id32, ACT.Copy).then_inc(idents, 1)

            def evac_hT(t):
                act.wait_ge(hT_psum, t + 1)
                nc.scalar.activation(hT[:, t % 2].rearrange("p k n -> p (k n)"), bank(2 + t % 2, D), ACT.Copy).then_inc(hT_ready, 1)

            def evac_v(t):
                act.wait_ge(qkv_psum, t + 1)
                act.wait_ge(rope_prod, t + 1)
                if t == 0:
                    act.wait_ge(pool_init, 3)
                nc.scalar.activation(vst[:, t, :, 0:HD],
                                     bank(6 + t % 2)[:, NQK * HD:QKV].rearrange("p (k d) -> p k d", d=HD),
                                     ACT.Copy).then_inc(v_ready, 1)

            def split0(t):
                act.wait_ge(roped, t + 1)
                src = rq[:, t % 4, 0:NH * HD].rearrange("p (h d) -> p h d", d=HD).unsqueeze(2)
                nc.scalar.activation(part[:, t % 4, 0:NH, 0:3, :], src.broadcast_to([P, NH, 3, HD]),
                                     ACT.Copy).then_inc(p0_ready, 1)

            def split1(t):
                act.wait_ge(r1_ready, t + 1)
                src = r1[:, t % 4, 0:NH * HD].rearrange("p (h d) -> p h d", d=HD).unsqueeze(2)
                nc.scalar.activation(part[:, t % 4, 0:NH, 3:5, :], src.broadcast_to([P, NH, 2, HD]),
                                     ACT.Copy).then_inc(p1_ready, 1)

            def evac_q(b, i):
                act.wait_ge(stack_psum, 5 * b + i + 1)
                half, qt = i % 2, i // 2
                nc.scalar.activation(qs[0:SLOT, b % 2, 8 * half:8 * half + 8, qt * P:(qt + 1) * P],
                                     ps[0:SLOT, i, :].bitcast(BF16).rearrange("p (h n) -> p h n", n=P),
                                     ACT.Copy).then_inc(stack_act, 1)

            def evac_oT(b, qt):
                act.wait_ge(oT_psum, 2 * b + qt + 1)
                nc.scalar.activation(oT[:, qt].rearrange("p k n -> p (k n)"), proj_bank(b, qt), ACT.Copy).then_inc(oT_ready, 1)

            def evac_ot(b, half):
                act.wait_ge(pv_done, 8 * b + 4 * half + 4)
                if b >= 1 and half == 0:
                    act.wait_ge(o_psum, 2 * b)
                nc.scalar.activation(ot[:, 2 * half:2 * half + 2, :].rearrange("p k s -> p (k s)"),
                                     bank(6), ACT.Copy).then_inc(ot_ready, 1)

            def exps(b, v):
                n = 8 * b + v
                act.wait_ge(score_psum, n + 1)
                if n >= 3:
                    act.wait_ge(pv_done, n - 2)
                src = ps[:, 2 * (n % 2):2 * (n % 2) + 2, :].rearrange("p a s -> p (a s)")
                nc.scalar.activation(pt[:, n % 3].rearrange("p r s -> p (r s)"), src, ACT.Exp,
                                     scale=float(HD) ** -0.5).then_inc(exp_done, 1)

            def split_h2(b, qt):
                t = 2 * b + qt
                act.wait_ge(h2T_psum, t + 1)
                nc.scalar.activation(h2T[:, 0, :, t * P:(t + 1) * P],
                                     h2_bank(b, qt), ACT.Copy).then_inc(h2hi, 1)

            def weight_sums():
                for i, wn in enumerate((w1n, w3n, w2n)):
                    n = HC if i < 2 else P
                    act.wait_ge(in_w[i], 32 if i < 2 else 16)
                    if i == 0:
                        act.wait_ge(dve_pad, 4)
                    else:
                        act.wait_ge(wsum_ready, i)
                    src = wn[:, :, :].rearrange("p c d -> p (c d)")
                    m = src.shape[1]
                    nc.scalar.activation(wabs[0:n, 0:m], src, ACT.Abs,
                                         accum_out=wsum[0:n, i:i + 1]).then_inc(wsum_ready, 1)

            def evac_wT(w):
                for k in range(KC):
                    act.wait_ge(wT_psum, 2 * w + k + 1)
                    nc.scalar.activation((w1T, w3T)[w][:, k, :], bank(6 + k).bitcast(F16)[:, 0:HP], ACT.Copy,
                                         scale=1.0 if w == 0 else W3SHIFT).then_inc(wT_act, 1)

            def tanh(n):
                act.wait_ge(up_psum, n + 1)
                if n == 0:
                    act.wait_ge(scale_ready, 4)
                if n >= 3:
                    act.wait_ge(g_ready, n - 2)
                nc.scalar.activation(u[:, n % 3, :], ps[0:HC, up_bank(n), 0:S], ACT.Tanh,
                                     scale=sgate[0:HC, :]).then_inc(tanh_done, 1)

            def gate_hi(n):
                act.wait_ge(g_ready, n + 1)
                nc.scalar.activation(gT[:, 0, n, :], g[:, n % 3, :], ACT.Copy).then_inc(ghi, 1)

            evac_hT(0)
            evac_hT(1)
            for t in range(2):
                evac_v(t)
                split0(t)
                split1(t)
            evac_hT(2)
            evac_hT(3)
            evac_q(0, 0)
            evac_q(0, 2)
            for t in range(2, 4):
                evac_v(t)
                split0(t)
                split1(t)
            evac_q(1, 0)
            evac_q(1, 2)
            weight_sums()
            for b in range(NB):
                t = 2 * b + 4
                if t < NT:
                    evac_hT(t)
                    evac_hT(t + 1)
                if b >= 1:
                    evac_oT(b - 1, 0)
                    evac_oT(b - 1, 1)
                if b >= 2:
                    evac_wT(b - 2)
                for v in range(8):
                    exps(b, v)
                    if b == NB - 1:
                        for n in range(first_unit(v), first_unit(v + 1)):
                            if n >= 1:
                                gate_hi(n - 1)
                            tanh(n)
                    if t < NT:
                        if v == 0:
                            evac_v(t)
                        if v == 1:
                            evac_v(t + 1)
                            split0(t)
                        if v == 2:
                            split1(t)
                        if v == 3:
                            split0(t + 1)
                        if v == 5:
                            split1(t + 1)
                    if v == 4:
                        evac_ot(b, 0)
                    if b >= 1 and v == (3 if b == NB - 1 else 5):
                        split_h2(b - 1, 0)
                    if b >= 1 and v == (5 if b == NB - 1 else 7):
                        split_h2(b - 1, 1)
                evac_ot(b, 1)
                if b + 2 < NB:
                    evac_q(b + 2, 0)
                    evac_q(b + 2, 2)
            b, n = NB - 1, 2 * CH
            gate_hi(n - 1)
            tanh(n)
            evac_oT(b, 0)
            evac_oT(b, 1)
            gate_hi(n)
            for i in range(1, 4):
                tanh(n + i)
                gate_hi(n + i)
            split_h2(b, 0)
            split_h2(b, 1)
            tanh(n + 4)
            for n in range(2 * CH + 5, NU):
                tanh(n)
                gate_hi(n - 1)
            gate_hi(NU - 1)

        @block.vector
        def _(dve):
            nc.vector.memset(w1n[96:HC, CH - 1, :], 0.0).then_inc(dve_pad, 1)
            nc.vector.memset(w3n[96:HC, CH - 1, :], 0.0).then_inc(dve_pad, 1)
            nc.vector.memset(w2n[:, :, HID:HP], 0.0).then_inc(dve_pad, 1)
            nc.vector.memset(wsum[:, :], 0.0).then_inc(dve_pad, 1)
            steps = [0]

            def chain(ins):
                steps[0] += 1
                ins.then_inc(dve_step, 1)
                dve.wait_ge(dve_step, steps[0])

            def stats(src, st, mv, b, signal):
                for qt in range(2):
                    ins = nc.vector.bn_stats(st[:, 2 * b + qt, :], src[:, 2 * b + qt, :])
                    ins.then_inc(dve_step, 1)
                    steps[0] += 1
                dve.wait_ge(dve_step, steps[0])
                for qt in range(2):
                    last = nc.vector.bn_aggr(mv[:, 2 * b + qt, :], st[:, 2 * b + qt, :])
                    if qt == 0:
                        last.then_inc(dve_step, 1)
                        steps[0] += 1
                last.then_inc(signal, 1)

            def norm1(b):
                dve.wait_ge(rstd1, b + 1)
                for qt in range(2):
                    t = 2 * b + qt
                    nc.vector.tensor_scalar(hn[:, t, :], x_sb[:, t, :], mv1[:, t, 0:1], rs1[:, t, 1:2],
                                            ALU.subtract, ALU.mult).then_inc(normed1, 1)

            def rope(t):
                i, qt = t % 4, t % 2
                if t == 0:
                    dve.wait_ge(in_cst, 16)
                dve.wait_ge(qkv_psum, t + 1)
                qk = bank(6 + t % 2)[:, 0:NQK * HD].rearrange("p (h f e) -> p h f e", f=HD // 2, e=2)
                c = cos[:, qt].unsqueeze(1).broadcast_to([P, NQK, HD])
                s = sin[:, qt].rearrange("p (f e) -> p f e", e=2).unsqueeze(1).broadcast_to([P, NQK, HD // 2, 2])
                nc.vector.tensor_tensor(ra[:, i].rearrange("p (h d) -> p h d", d=HD),
                                        bank(6 + t % 2)[:, 0:NQK * HD].rearrange("p (h d) -> p h d", d=HD), c,
                                        ALU.mult)
                nc.vector.tensor_tensor(rb[:, i].rearrange("p (h f e) -> p h f e", f=HD // 2, e=2), qk[:, :, :, ::-1], s,
                                        ALU.mult).then_inc(rope_prod, 1)

            def evac_q(b, i):
                dve.wait_ge(stack_psum, 5 * b + i + 1)
                half, qt = i % 2, i // 2
                nc.vector.tensor_copy(qs[0:SLOT, b % 2, 8 * half:8 * half + 8, qt * P:(qt + 1) * P],
                                      ps[0:SLOT, i, :].bitcast(BF16).rearrange("p (h n) -> p h n", n=P)
                                      ).then_inc(stack_dve, 1)

            def evac_k(b):
                dve.wait_ge(stack_psum, 5 * b + 5)
                nc.vector.tensor_copy(ks[0:SLOT, b % 2, :, :].rearrange("p k s -> p (k s)"),
                                      ps[0:SLOT, 7, :].bitcast(BF16)).then_inc(stack_dve, 1)

            def row_max(b, w):
                qt, kv, rp = w // 8, (w // 2) % 4, w % 2
                dve.wait_ge(max_psum, 16 * b + w + 1)
                if w == 0 and b >= 1:
                    dve.wait_ge(nms_ready, b)
                nc.vector.tensor_reduce(nmx[:, qt, 2 * rp * NKV + kv:(2 * rp + 1) * NKV + kv + 1:NKV],
                                        bank(4 + w % 2).rearrange("p (r s) -> p r s", r=2),
                                        axis=AX.X, op=ALU.max, negate=True).then_inc(max_done, 1)

            def split_max(b):
                dve.wait_ge(max_done, 16 * b + 16)
                if b >= 1:
                    dve.wait_ge(nmT_psum, b)
                chain(nc.vector.tensor_copy(nms[:, :, 0, :], nmx[:, :, :]))
                chain(nc.vector.tensor_tensor(nmr[:, :, :], nmx[:, :, :], nms[:, :, 0, :], ALU.subtract))
                chain(nc.vector.tensor_copy(nms[:, :, 1, :], nmr[:, :, :]))
                nc.vector.tensor_tensor(nms[:, :, 2, :], nmr[:, :, :], nms[:, :, 1, :],
                                        ALU.subtract).then_inc(nms_ready, 1)

            def evac_max(b):
                dve.wait_ge(nmT_psum, b + 1)
                if b >= 2:
                    dve.wait_ge(mrows, 16 * MROW * (b - 1))
                nc.vector.tensor_copy(nmT[:, b % 2, :], ps[0:MROW * NH, 5, 0:S // 2].bitcast(BF16)).then_inc(nmT_ready, 1)

            def normalise(b, qt):
                dve.wait_ge(o_psum, 2 * b + qt + 1)
                if b >= 1:
                    dve.wait_ge(oT_psum, 2 * b - 1 + qt)
                o = bank(qt).rearrange("p (k r c) -> p k r c", k=NKV, r=REP)
                rd = rden[:, qt].rearrange("p (k r) -> p k r", k=NKV)
                chain(nc.vector.reciprocal(rd, o[:, :, :, HD]))
                nc.vector.tensor_tensor(on[:, qt].rearrange("p r k d -> p k r d"), o[:, :, :, 0:HD],
                                        rd.unsqueeze(3).broadcast_to([P, NKV, REP, HD]),
                                        ALU.mult).then_inc(on_ready, 1)

            def residual(b, qt):
                t = 2 * b + qt
                dve.wait_ge(wo_psum, t + 1)
                nc.vector.tensor_tensor(x1[:, t, :], x_sb[:, t, :], proj_bank(b, qt), ALU.add).then_inc(x1_ready, 1)

            def norm2(b):
                dve.wait_ge(rstd2, b + 1)
                for qt in range(2):
                    t = 2 * b + qt
                    if b >= 1:
                        dve.wait_ge(h2T_psum, t - 1)
                    nc.vector.tensor_scalar(h2[:, qt, :], x1[:, t, :], mv2[:, t, 0:1], rs2[:, t, 1:2],
                                            ALU.subtract, ALU.mult).then_inc(h2_ready, 1)

            def split_h2(b, qt):
                t = 2 * b + qt
                dve.wait_ge(h2hi, t + 1)
                sl = slice(t * P, (t + 1) * P)
                nc.vector.tensor_tensor(h2T[:, 1, :, sl], h2_bank(b, qt),
                                        h2T[:, 0, :, sl], ALU.subtract).then_inc(h2lo, 1)

            def layer_norm2_stats(b):
                dve.wait_ge(x1_ready, 2 * b + 2)
                stats(x1, st2, mv2, b, var2)

            def scales():
                dve.wait_ge(wtot_psum, 1)
                nc.vector.tensor_scalar(scl[:, :], bank(4, 3), 1.0 / (HID * D), None, ALU.mult).then_inc(scale_ready, 1)
                dve.wait_ge(scale_ready, 1)
                nc.vector.tensor_scalar(thr[:, :], scl[:, :], 0.5, None, ALU.mult).then_inc(scale_ready, 1)
                nc.vector.tensor_scalar(nthr[:, :], scl[:, :], -0.5, None, ALU.mult).then_inc(scale_ready, 1)
                nc.vector.tensor_scalar(sgate[:, :], scl[:, 0:1], -0.5, None, ALU.mult).then_inc(scale_ready, 1)
                chain(nc.vector.tensor_tensor(sout[:, 0:1], scl[:, 0:1], scl[:, 1:2], ALU.mult))
                chain(nc.vector.scalar_tensor_tensor(sout[:, 1:2], sout[:, 0:1], -0.5 / W3SHIFT, scl[:, 2:3],
                                                     ALU.mult, ALU.mult))

            def evac_w2T():
                for k in range(KC):
                    dve.wait_ge(wT_psum, 4 + k + 1)
                    nc.vector.tensor_copy(w2T[:, :, k * P:(k + 1) * P],
                                          ps[0:HC, 2 + k, :].bitcast(F16)[:, 0:CH * P].rearrange("p (c n) -> p c n", c=CH)
                                          ).then_inc(wT_dve, 1)

            def gate(n):
                yb = ps[0:HC, up_bank(n), :]
                dve.wait_ge(tanh_done, n + 1)
                if n >= 3:
                    dve.wait_ge(glo, n - 2)
                chain(nc.vector.scalar_tensor_tensor(uv[:, n % 3, :], u[:, n % 3, :], 1.0, yb[:, 0:S],
                                                     ALU.add, ALU.mult))
                nc.vector.tensor_tensor(g[:, n % 3, :], uv[:, n % 3, :], yb[:, S:2 * S], ALU.mult).then_inc(g_ready, 1)

            def output(n):
                dve.wait_ge(down_psum, n + 1)
                t = 2 * n if n < NB - 1 else NB - 1 + n
                e = t + 2 if n < NB - 1 else t + 1
                src = ps[:, (7, 2, 7, 2, 3)[n], 0:(e - t) * D].rearrange("p (t d) -> p t d", d=D)
                nc.vector.scalar_tensor_tensor(y[:, t:e, :], src, sout[:, 1:2], x1[:, t:e, :],
                                               ALU.mult, ALU.add).then_inc(y_ready, 1)

            for b in range(2):
                dve.wait_ge(in_x[b], 16)
                stats(x_sb, st1, mv1, b, var1)
                norm1(b)
            rope(0)
            rope(1)
            for b in range(2, NB):
                dve.wait_ge(in_x[b], 16)
                stats(x_sb, st1, mv1, b, var1)
            evac_q(0, 1)
            evac_q(0, 3)
            evac_k(0)
            rope(2)
            rope(3)
            norm1(2)
            norm1(3)
            for w in range(16):
                row_max(0, w)
                if w == 9:
                    evac_q(1, 1)
                    evac_q(1, 3)
                    evac_k(1)
            split_max(0)
            evac_max(0)

            for b in range(NB):
                t = 2 * b + 4
                if b >= 1:
                    normalise(b - 1, 0)
                    normalise(b - 1, 1)
                if t < NT:
                    rope(t)
                    rope(t + 1)
                if b == 0:
                    scales()
                if b == NB - 1:
                    evac_w2T()
                if b >= 1:
                    residual(b - 1, 0)
                    residual(b - 1, 1)
                    layer_norm2_stats(b - 1)
                for v in range(8):
                    if b + 1 < NB:
                        row_max(b + 1, 2 * v)
                        row_max(b + 1, 2 * v + 1)
                    if b >= 1 and v == 0:
                        norm2(b - 1)
                    if b == NB - 1:
                        for n in range(first_unit(v), first_unit(v + 1)):
                            gate(n)
                    if b >= 1 and v == (3 if b == NB - 1 else 6):
                        split_h2(b - 1, 0)
                    if b >= 1 and v == (5 if b == NB - 1 else 7):
                        split_h2(b - 1, 1)
                if b + 1 < NB:
                    split_max(b + 1)
                if b + 2 < NB:
                    evac_q(b + 2, 1)
                    evac_q(b + 2, 3)
                    evac_k(b + 2)
                if b + 1 < NB:
                    evac_max(b + 1)
            b, n = NB - 1, 2 * CH
            normalise(b, 0)
            normalise(b, 1)
            output(0)
            gate(n)
            gate(n + 1)
            residual(b, 0)
            residual(b, 1)
            layer_norm2_stats(b)
            gate(n + 2)
            norm2(b)
            gate(n + 3)
            output(1)
            split_h2(b, 0)
            split_h2(b, 1)
            for n in range(2 * CH + 4, NU):
                gate(n)
                if n == NU - 3:
                    output(2)
            output(3)
            output(4)

        @block.tensor
        def _(pe):
            def tr_h(t):
                pe.wait_ge(normed1, t + 1)
                if t == 0:
                    pe.wait_ge(in_cst, 16)
                if t >= 2:
                    pe.wait_ge(hT_ready, t - 1)
                for k in range(KC):
                    last = nc.tensor.transpose(bank(2 + t % 2)[:, k * P:(k + 1) * P], hn[:, t, k * P:(k + 1) * P], id32)
                last.then_inc(hT_psum, 1)

            def project(t):
                pe.wait_ge(hT_ready, t + 1)
                if t == 0:
                    pe.wait_ge(in_wqkv, 48)
                if t >= 2:
                    pe.wait_ge(v_ready, t - 1)
                if t >= 3 and t % 2:
                    pe.wait_ge(stack_dve, 3 * (t - 1) // 2)
                for k in range(KC):
                    last = nc.tensor.matmul(bank(6 + t % 2, QKV), hT[:, t % 2, k, :], wqkv_sb[:, k, :],
                                            start=(k == 0), stop=(k == KC - 1))
                last.then_inc(qkv_psum, 1)

            def stack_q(b, i):
                half, qt = i % 2, i // 2
                t = 2 * b + qt
                pe.wait_ge(parts_ready, 2 * t + 2)
                if t == 0:
                    pe.wait_ge(idents, 1)
                dst = ps[0:SLOT, i, :].bitcast(BF16)
                for j in range(8):
                    last = nc.tensor.transpose(dst[:, j * P:(j + 1) * P],
                                               part[:, t % 4, 8 * half + j].rearrange("p s d -> p (s d)"), idb[:, :])
                last.then_inc(stack_psum, 1)

            def stack_k(b):
                dst = ps[0:SLOT, 7, :].bitcast(BF16)
                for kv in range(NKV):
                    for kt in range(2):
                        j = 2 * kv + kt
                        last = nc.tensor.transpose(dst[:, j * P:(j + 1) * P],
                                                   part[:, (2 * b + kt) % 4, NH + kv].rearrange("p s d -> p (s d)"), idb[:, :])
                last.then_inc(stack_psum, 1)

            def max_scores(b, w):
                qt, kv, rp = w // 8, (w // 2) % 4, w % 2
                n = 16 * b + w
                if w == 0:
                    pe.wait_ge(stack_act, 2 * b + 2)
                    pe.wait_ge(stack_dve, 3 * b + 3)
                if w == 0 and b >= 1:
                    pe.wait_ge(nmT_ready, b)
                if w == 0 and b >= 2:
                    pe.wait_ge(x1_ready, 2 * (b - 1))
                if n == 16:
                    pe.wait_ge(scale_ready, 1)
                if n >= 2:
                    pe.wait_ge(max_done, n - 1)
                for r in range(2):
                    last = nc.tensor.matmul(bank(4 + w % 2)[:, r * S:(r + 1) * S],
                                            qs[0:SLOT, b % 2, (2 * rp + r) * NKV + kv, qt * P:(qt + 1) * P],
                                            ks[0:SLOT, b % 2, kv, :], start=True, stop=True)
                last.then_inc(max_psum, 1)

            def scores(b, v):
                n, kv, kt = 8 * b + v, v // 2, v % 2
                if v == 0:
                    pe.wait_ge(mrows, 16 * MROW * (b + 1))
                    pe.wait_ge(pool_init, 4)
                if v == 0:
                    pe.wait_ge(stack_act, 2 * min(b + 2, NB))
                    pe.wait_ge(stack_dve, 3 * min(b + 2, NB) - 1)
                    pe.wait_ge(hT_ready, min(2 * b + 6, NT))
                    if b >= 1:
                        pe.wait_ge(on_ready, 2 * b)
                if b == NB - 1 and v == 1:
                    pe.wait_ge(wT_dve, 2)
                if n >= 2:
                    pe.wait_ge(exp_done, n - 1)
                for h in range(2):
                    last = nc.tensor.matmul(bank(2 * (n % 2) + h), ks[0:SLOT + MROW, b % 2, kv, kt * P:(kt + 1) * P],
                                            qs[0:SLOT + MROW, b % 2, 2 * h * NKV + kv:(2 * h + 1) * NKV + kv + 1:NKV, :],
                                            start=True, stop=True)
                last.then_inc(score_psum, 1)

            def pv(b, v):
                n, kv, kt = 8 * b + v, v // 2, v % 2
                pe.wait_ge(exp_done, n + 1)
                if v == 0:
                    pe.wait_ge(v_ready, min(2 * b + 5, NT))
                    if b >= 1:
                        pe.wait_ge(ot_ready, 2 * b)
                    if b >= 2:
                        pe.wait_ge(wT_act, 2 * (b - 1))
                if v == 4:
                    pe.wait_ge(ot_ready, 2 * b + 1)
                for r in range(REP):
                    last = nc.tensor.matmul(ps[VW * r:VW * (r + 1), 6, (kv % 2) * S:(kv % 2 + 1) * S],
                                            vst[:, 2 * b + kt, kv, :], pt[:, n % 3, r, :],
                                            start=(kt == 0), stop=(kt == 1))
                last.then_inc(pv_done, 1)

            def tr_max(b):
                pe.wait_ge(nms_ready, b + 1)
                dst = ps[0:MROW * NH, 5, 0:S // 2].bitcast(BF16)
                for qt in range(2):
                    last = nc.tensor.transpose(dst[:, qt * P:(qt + 1) * P], nms[:, qt].rearrange("p m h -> p (m h)"), idb[:, :])
                last.then_inc(nmT_psum, 1)

            def tr_o(b, qt):
                if qt == 0:
                    pe.wait_ge(ot_ready, 2 * b + 2)
                    pe.wait_ge(stack_act, 2 * min(b + 3, NB))
                    pe.wait_ge(stack_dve, 3 * min(b + 3, NB) - 1)
                for kv in range(NKV):
                    last = nc.tensor.transpose(bank(qt)[:, kv * P:(kv + 1) * P], ot[:, kv, qt * P:(qt + 1) * P], id32)
                last.then_inc(o_psum, 1)

            def tr_on(b, qt):
                pe.wait_ge(on_ready, 2 * b + qt + 1)
                if b + 1 < NB:
                    pe.wait_ge(max_done, 16 * (b + 2))
                    pe.wait_ge(nmT_ready, b + 2)
                o = on[:, qt].rearrange("p r k d -> p (r k d)")
                for k in range(KC):
                    last = nc.tensor.transpose(proj_bank(b, qt)[:, k * P:(k + 1) * P], o[:, k * P:(k + 1) * P], id32)
                last.then_inc(oT_psum, 1)

            def out_proj(b, qt):
                pe.wait_ge(oT_ready, 2 * b + qt + 1)
                if b == 0 and qt == 0:
                    pe.wait_ge(in_wo, 16)
                for k in range(KC):
                    last = nc.tensor.matmul(proj_bank(b, qt), oT[:, qt, k, :], wo_sb[:, k, :],
                                            start=(k == 0), stop=(k == KC - 1))
                last.then_inc(wo_psum, 1)

            def tr_h2(b, qt):
                pe.wait_ge(h2_ready, 2 * b + qt + 1)
                for k in range(KC):
                    last = nc.tensor.transpose(h2_bank(b, qt)[:, k, :], h2[:, qt, k * P:(k + 1) * P], id32)
                last.then_inc(h2T_psum, 1)

            def tr_w(w, k, bk):
                pe.wait_ge(tern_ready, w + 1)
                for c in range(CH):
                    if w < 2:
                        last = nc.tensor.transpose(bank(bk).bitcast(F16)[:, c * HC:(c + 1) * HC],
                                                   tern[0:HC, w, c * D + k * P:c * D + (k + 1) * P], idh[0:HC, 0:HC])
                    else:
                        last = nc.tensor.transpose(ps[0:HC, bk, :].bitcast(F16)[:, c * P:(c + 1) * P],
                                                   tern[:, 2, k * HP + c * HC:k * HP + (c + 1) * HC], idh[:, :])
                last.then_inc(wT_psum, 1)

            def up(n):
                f, c = n // CH, n % CH
                if c == 0:
                    pe.wait_ge(h2lo, 2 * f + 2)
                if n == 0:
                    pe.wait_ge(wT_act, 4)
                    pe.wait_ge(x1_ready, 2 * NB - 2)
                if 2 <= n < NU - CH + 2:
                    pe.wait_ge(g_ready, n - 1)
                if n == NU - CH + 2:
                    pe.wait_ge(h2lo, 2 * NB)
                if n >= NU - CH + 3:
                    pe.wait_ge(g_ready, n - 2)
                for m, wT in enumerate((w1T, w3T)):
                    for i in range(2 * KC):
                        k, part_ = i // 2, i % 2
                        last = nc.tensor.matmul(ps[0:HC, up_bank(n), m * S:(m + 1) * S], wT[:, k, c * HC:(c + 1) * HC],
                                                h2T[:, part_, k, f * S:(f + 1) * S],
                                                start=(i == 0), stop=(i == 2 * KC - 1))
                last.then_inc(up_psum, 1)

            def down_chunk(t, c):
                f, j = t // 2, t % 2
                for h in range(2):
                    last = nc.tensor.matmul(down_bank(t), gT[:, h, f * CH + c, j * P:(j + 1) * P], w2T[:, c, :],
                                            start=(c == 0 and h == 0), stop=(c == CH - 1 and h == 1))
                return last

            def down(t):
                pe.wait_ge(glo, CH * (t // 2 + 1))
                if t == 0:
                    pe.wait_ge(wT_dve, 2)
                    pe.wait_ge(h2lo, 2 * NB - 2)
                if t == 4:
                    pe.wait_ge(y_ready, 1)
                for c in range(CH):
                    last = down_chunk(t, c)
                if t % 2:
                    last.then_inc(down_psum, 1)

            tr_h(0)
            tr_h(1)
            project(0)
            project(1)
            tr_h(2)
            tr_h(3)
            stack_q(0, 0)
            stack_q(0, 1)
            pe.wait_ge(hT_ready, 4)
            stack_q(0, 2)
            stack_q(0, 3)
            pe.wait_ge(v_ready, 2)
            stack_k(0)
            project(2)
            project(3)
            for w in range(16):
                max_scores(0, w)
                if w == 7:
                    for i in range(4):
                        stack_q(1, i)
                    pe.wait_ge(v_ready, 4)
                    stack_k(1)
            tr_max(0)

            for b in range(NB):
                t = 2 * b + 4
                if b >= 1:
                    tr_o(b - 1, 0)
                    tr_o(b - 1, 1)
                if t < NT:
                    pe.wait_ge(stack_act, 2 * (b + 2))
                    pe.wait_ge(stack_dve, 3 * (b + 2) - 1)
                    tr_h(t)
                    tr_h(t + 1)
                if b >= 1:
                    tr_on(b - 1, 0)
                    tr_on(b - 1, 1)
                if t < NT:
                    if b >= 1:
                        pe.wait_ge(ot_ready, 2 * b)
                    project(t)
                    project(t + 1)
                if b == 0:
                    pe.wait_ge(wsum_ready, 3)
                    pe.wait_ge(pool_init, 5)
                    pe.wait_ge(max_done, 16)
                    nc.tensor.matmul(bank(4, 3), ones[:, :], wsum[:, :], start=True, stop=True).then_inc(wtot_psum, 1)
                if b == 2:
                    pe.wait_ge(idents, 2)
                if b >= 2:
                    pe.wait_ge(ot_ready, 2 * b)
                    tr_w(b - 2, 0, 6)
                    pe.wait_ge(stack_dve, 3 * NB)
                    pe.wait_ge(h2lo, 2 * b - 2)
                    tr_w(b - 2, 1, 7)
                if b == NB - 1:
                    tr_w(2, 0, 2)
                    tr_w(2, 1, 3)
                if b >= 1:
                    out_proj(b - 1, 0)
                    out_proj(b - 1, 1)
                for v in range(8):
                    scores(b, v)
                    if b + 1 < NB:
                        max_scores(b + 1, 2 * v)
                        max_scores(b + 1, 2 * v + 1)
                    if b == NB - 1:
                        for n in range(first_unit(v), first_unit(v + 1)):
                            up(n)
                    if v >= 1:
                        pv(b, v - 1)
                    if b >= 1 and v == (2 if b == NB - 1 else 3):
                        pe.wait_ge(v_ready, min(2 * b + 6, NT))
                        pe.wait_ge(stack_dve, 3 * min(b + 2, NB))
                        if b >= 2:
                            pe.wait_ge(h2lo, 2 * b - 2)
                            pe.wait_ge(wT_act, 2 * (b - 1))
                        tr_h2(b - 1, 0)
                    if b >= 1 and v == (4 if b == NB - 1 else 6):
                        pe.wait_ge(h2lo, 2 * b - 1)
                        tr_h2(b - 1, 1)
                    if b == NB - 1 and v >= 6:
                        down(v - 6)
                pv(b, 7)
                if b + 2 < NB:
                    pe.wait_ge(exp_done, 8 * b + 8)
                    for i in range(4):
                        stack_q(b + 2, i)
                    if b >= 1:
                        pe.wait_ge(h2lo, 2 * b)
                    else:
                        pe.wait_ge(v_ready, 6)
                    stack_k(b + 2)
                if b + 1 < NB:
                    tr_max(b + 1)
            b, n = NB - 1, 2 * CH
            tr_o(b, 0)
            tr_o(b, 1)
            up(n)
            tr_on(b, 0)
            tr_on(b, 1)
            up(n + 1)
            out_proj(b, 0)
            out_proj(b, 1)
            up(n + 2)
            down(2)
            up(n + 3)
            down(3)
            tr_h2(b, 0)
            tr_h2(b, 1)
            up(n + 4)
            up(n + 5)
            up(n + 6)
            up(n + 7)
            down(4)
            up(n + 8)
            down(5)
            pe.wait_ge(y_ready, 2)
            pe.wait_ge(x1_ready, 2 * NB)
            for c in range(CH):
                if c < 3:
                    up(n + 9 + c)
                pe.wait_ge(glo, 3 * CH + c + 1)
                for t in (6, 7):
                    last = down_chunk(t, c)
                    if c == CH - 1:
                        last.then_inc(down_psum, 1)


_W = ("L0_attn_W_q", "L0_attn_W_k", "L0_attn_W_v", "L0_attn_W_o", "L0_ffn_w1", "L0_ffn_w3", "L0_ffn_w2")


def _constants():
    half = HD // 2
    freq = (np.float32(1.0) / np.float32(10000.0) ** (np.arange(half, dtype=np.float32) / np.float32(half))).astype(np.float32)
    ang = np.arange(S, dtype=np.float32)[:, None] * freq[None, :]
    c, s = np.cos(ang).astype(np.float32), np.sin(ang).astype(np.float32)
    cos = np.repeat(c, 2, axis=1)
    sin = np.stack([-s, s], axis=-1).reshape(S, HD)
    tiles = [a.reshape(2, P, HD).transpose(1, 0, 2).reshape(P, 2 * HD) for a in (cos, sin)]
    return np.ascontiguousarray(np.concatenate([np.eye(P, dtype=np.float32), *tiles], axis=1))


def kernel(**inputs):
    import concourse.bacc as bacc
    from concourse.bass_utils import run_bass_kernel_spmd

    nc = bacc.Bacc("TRN2", target_bir_lowering=False, num_devices=1)
    arrays = {"x": np.ascontiguousarray(inputs["L0_attn_x"]), "consts": _constants()}
    for name in _W:
        arrays[name] = np.ascontiguousarray(inputs[name])
    aps = {n: nc.dram_tensor(n, a.shape, mybir.dt.from_np(a.dtype), kind="ExternalInput").ap() for n, a in arrays.items()}
    out = nc.dram_tensor("out", (NB, S, D), F32, kind="ExternalOutput").ap()
    w = [aps[n] for n in _W]
    build(nc, aps["x"], w[0:3], w[3], w[4], w[5], w[6], aps["consts"], out)
    r = run_bass_kernel_spmd(nc, [arrays], core_ids=[0])
    return r.results[0]["out"]
```

```python
from contextlib import ExitStack

import numpy as np

import concourse.bass as bass
from concourse import mybir

F32 = mybir.dt.float32
BF16 = mybir.dt.bfloat16
F16 = mybir.dt.float16
ALU = mybir.AluOpType
ACT = mybir.ActivationFunctionType
AX = mybir.AxisListType

P = 128
NB, S, D = 4, 256, 256
NT = NB * S // P
HD, NKV, REP = 16, 4, 4
NH = NKV * REP
NQK = NH + NKV
QKV = D + 2 * NKV * HD
KC = D // P
HID = int(2 * D * 4 / 3)
CH = 6
HC = 114
HP = CH * HC
LAST = HID - (CH - 1) * HC
SLOT = 6 * HD
MROW = 3
EPS = 1e-5
UPS = (2, 1, 2, 1, 2, 1, 2, 1)
NU = NB * CH
MAX_LEAD = (4, 4, 4)
MAX_AT = ((1, 1, 2, 2, 2, 2, 2, 0), (1, 2, 1, 2, 2, 2, 2, 0), (1, 2, 1, 2, 2, 2, 2, 0))
WIDE = 16
W3SHIFT = 2.0 ** -6
WARM = 40
VW = 32


def build(nc, x, wqkv, wo, w1, w3, w2, consts, out):
    ctx = ExitStack()
    with ctx:
        def sb(name, shape, dt=F32):
            return ctx.enter_context(nc.sbuf_tensor(name, shape, dt))

        def sem(name):
            return ctx.enter_context(nc.semaphore(name))

        x_sb = sb("x_sb", [P, NT, D])
        x1 = sb("x1", [P, NT, D])
        wqkv_sb = sb("wqkv_sb", [P, KC, QKV])
        wo_sb = sb("wo_sb", [P, KC, D])
        cst = sb("cst", [P, P + 4 * HD])
        id32 = cst[:, 0:P]
        cos = cst[:, P:P + 2 * HD].rearrange("p (q d) -> p q d", q=2)
        sin = cst[:, P + 2 * HD:P + 4 * HD].rearrange("p (q d) -> p q d", q=2)
        idb = sb("idb", [P, P], BF16)
        idh = sb("idh", [P, P], F16)
        ones = sb("ones", [P, P])
        mhalf = sb("mhalf", [P, 2])
        st1 = sb("st1", [P, NT, 6])
        mv1 = sb("mv1", [P, NT, 2])
        rs1 = sb("rs1", [P, NT, 2])
        hn = sb("hn", [P, NT, D])
        hT = sb("hT", [P, 2, KC, P])
        ra = sb("ra", [P, 4, NQK * HD])
        rb = sb("rb", [P, 4, NQK * HD])
        rq = sb("rq", [P, 4, NQK * HD])
        r1 = sb("r1", [P, 4, NQK * HD])
        part = sb("part", [P, 4, NQK, 6, HD], BF16)
        vst = sb("vst", [P, NT, NKV, VW])
        qs = sb("qs", [P, 2, NH, S], BF16)
        ks = sb("ks", [P, 2, NKV, S], BF16)
        nmx = sb("nmx", [P, 2, NH])
        nmr = sb("nmr", [P, 2, NH])
        nms = sb("nms", [P, 2, MROW, NH], BF16)
        nmT = sb("nmT", [MROW * NH, 2, S], BF16)
        pt = sb("pt", [P, 3, REP, S])
        ot = sb("ot", [P, NKV, S])
        rden = sb("rden", [P, 2, NH])
        on = sb("on", [P, 2, REP, NKV, HD])
        oT = sb("oT", [P, 2, KC, P])
        st2 = sb("st2", [P, NT, 6])
        mv2 = sb("mv2", [P, NT, 2])
        rs2 = sb("rs2", [P, NT, 2])
        h2 = sb("h2", [P, 2, D])
        h2T = sb("h2T", [P, 2, KC, NB * S], F16)
        w1n = sb("w1n", [HC, CH, D])
        w3n = sb("w3n", [HC, CH, D])
        w2n = sb("w2n", [P, KC, HP])
        tern = sb("tern", [P, 3, CH * D], F16)
        tpos = sb("tpos", [P, CH * D], F16)
        tneg = sb("tneg", [P, CH * D], F16)
        wabs = sb("wabs", [P, CH * D], BF16)
        wsum = sb("wsum", [P, 3])
        scl = sb("scl", [P, 3])
        thr = sb("thr", [P, 3])
        nthr = sb("nthr", [P, 3])
        sgate = sb("sgate", [P, 1])
        sout = sb("sout", [P, 2])
        w1T = sb("w1T", [P, KC, HP], F16)
        w3T = sb("w3T", [P, KC, HP], F16)
        w2T = sb("w2T", [HC, CH, D], F16)
        u = sb("u", [HC, 4, S])
        uv = sb("uv", [HC, 4, S])
        g = sb("g", [HC, 4, S])
        gT = sb("gT", [HC, 2, NU, S], F16)
        y = hn

        ps = ctx.enter_context(nc.psum_tensor("ps", [P, 8, 512], F32))

        def bank(i, n=512):
            return ps[:, i, 0:n]

        in_x = [sem(f"in_x{b}") for b in range(NB)]
        in_cst, in_wqkv, in_wo = sem("in_cst"), sem("in_wqkv"), sem("in_wo")
        in_w = [sem(f"in_w{i}") for i in range(3)]
        pool_init, dve_pad, idents = sem("pool_init"), sem("dve_pad"), sem("idents")
        dve_step, pool_step = sem("dve_step"), sem("pool_step")
        var1, rstd1, normed1 = sem("var1"), sem("rstd1"), sem("normed1")
        hT_psum, hT_ready, qkv_psum = sem("hT_psum"), sem("hT_ready"), sem("qkv_psum")
        rope_prod, v_ready, roped = sem("rope_prod"), sem("v_ready"), sem("roped")
        p0k_ready, p1k_ready = sem("p0k_ready"), sem("p1k_ready")
        p0_ready, r1_ready, p1_ready = sem("p0_ready"), sem("r1_ready"), sem("p1_ready")
        q_parts, k_parts = sem("q_parts"), sem("k_parts")
        stack_psum, stack_act, stack_dve = sem("stack_psum"), sem("stack_act"), sem("stack_dve")
        max_psum, max_done, nms_ready = sem("max_psum"), sem("max_done"), sem("nms_ready")
        nmT_psum, nmT_ready, mrows = sem("nmT_psum"), sem("nmT_ready"), sem("mrows")
        score_psum, exp_done, pv_done = sem("score_psum"), sem("exp_done"), sem("pv_done")
        ot_ready, o_psum, on_ready = sem("ot_ready"), sem("o_psum"), sem("on_ready")
        oT_psum, oT_ready, wo_psum, x1_ready = sem("oT_psum"), sem("oT_ready"), sem("wo_psum"), sem("x1_ready")
        var2, rstd2, h2_ready, h2T_psum = sem("var2"), sem("rstd2"), sem("h2_ready"), sem("h2T_psum")
        h2hi, h2lo = sem("h2hi"), sem("h2lo")
        wsum_ready, wtot_psum, scale_ready, tern_ready = sem("wsum_ready"), sem("wtot_psum"), sem("scale_ready"), sem("tern_ready")
        wT_psum, wT_act, wT_dve = sem("wT_psum"), sem("wT_act"), sem("wT_dve")
        up_psum, tanh_done, g_ready, ghi, glo = sem("up_psum"), sem("tanh_done"), sem("g_ready"), sem("ghi"), sem("glo")
        down_psum, y_ready, stored = sem("down_psum"), sem("y_ready"), sem("stored")

        def qkv_bank(t):
            return 6 if t in (0, 2, 4) else 7

        def proj_bank(b, qt):
            return bank((6, 3)[qt] if b == NB - 1 else 6 + qt, D)

        def up_bank(n):
            return 4 + n % 2 if n < WIDE else (4, 5, 6, 3)[n % 4]

        def down_bank(t):
            return bank((7, 2, 7)[t // 2])[:, (t % 2) * D:(t % 2 + 1) * D] if t < NT - 2 else bank((2, 1)[t % 2], D)

        def h2_bank(b, qt):
            return bank(qt if b == NB - 1 else 7, D).rearrange("p (k n) -> p k n", k=KC)

        def first_unit(v):
            return sum(UPS[:v])

        def max_units(b, v):
            first = MAX_LEAD[b] + sum(MAX_AT[b][:v])
            return range(first, first + MAX_AT[b][v])

        block = ctx.enter_context(nc.Block())

        @block.sync
        def _(sp):
            def load_x(b):
                sp.dma_start(x_sb[:, 2 * b:2 * b + 2, :],
                             x[b].rearrange("(t p) d -> p t d", p=P)).then_inc(in_x[b], 16)

            load_x(0)
            sp.dma_start(cst[:, :], consts).then_inc(in_cst, 16)
            for i, w in enumerate(wqkv):
                n0 = (0, D, D + NKV * HD)[i]
                sp.dma_start(wqkv_sb[:, :, n0:n0 + w.shape[1]],
                             w.rearrange("(k p) n -> p k n", p=P)).then_inc(in_wqkv, 16)
            for b in range(1, NB):
                load_x(b)
            sp.dma_start(wo_sb[:, :, :], wo.rearrange("(k p) n -> p k n", p=P)).then_inc(in_wo, 16)
            sp.wait_ge(dve_pad, 3)
            for i, (w, wn) in enumerate(((w1, w1n), (w3, w3n))):
                sp.dma_start(wn[:, 0:CH - 1, :],
                             w[0:(CH - 1) * HC, :].rearrange("(c p) d -> p c d", p=HC)).then_inc(in_w[i], 16)
                sp.dma_start(wn[0:LAST, CH - 1, :], w[(CH - 1) * HC:HID, :]).then_inc(in_w[i], 16)
            sp.dma_start(w2n[:, :, 0:HID], w2.rearrange("(k p) h -> p k h", p=P)).then_inc(in_w[2], 16)

            def max_rows(b):
                sp.wait_ge(nmT_ready, b + 1)
                for m in range(MROW):
                    sp.dma_start(qs[SLOT + m:SLOT + m + 1, b % 2, :, :],
                                 nmT[m * NH:(m + 1) * NH, b % 2, :]).then_inc(mrows, 16)

            for b in range(NB):
                max_rows(b)
            for b in range(NB - 1):
                sp.wait_ge(y_ready, b + 1)
                sp.dma_start(out[b].rearrange("(t p) d -> p t d", p=P), y[:, 2 * b:2 * b + 2, :]).then_inc(stored, 16)
            for qt in range(2):
                sp.wait_ge(y_ready, NB + qt)
                sp.dma_start(out[NB - 1, qt * P:(qt + 1) * P, :], y[:, NT - 2 + qt, :]).then_inc(stored, 16)
            sp.wait_ge(stored, 16 * (NB + 1))

        @block.gpsimd
        def _(pool):
            for n, (dst, value) in enumerate(((ones[:, :], 1.0), (mhalf[:, :], -0.5), (vst[:, :, :, :], 0.0),
                                              (vst[:, :, :, HD:HD + 1], 1.0),
                                              (ks[SLOT:SLOT + MROW, :, :, :], 1.0))):
                nc.gpsimd.memset(dst, value).then_inc(pool_init, 1)
                pool.wait_ge(pool_init, n + 1)
            steps = [0]

            def chain(ins):
                steps[0] += 1
                ins.then_inc(pool_step, 1)
                pool.wait_ge(pool_step, steps[0])

            def rsqrt(rs, var, b):
                sl = slice(2 * b, 2 * b + 2)
                chain(nc.gpsimd.tensor_scalar(rs[:, sl, 0], var[:, sl, 1], EPS, None, ALU.add))
                return nc.gpsimd.tensor_tensor(rs[:, sl, 1], rs[:, sl, 0], mhalf[:, :], ALU.pow)

            def rsqrt1(b):
                pool.wait_ge(var1, b + 1)
                rsqrt(rs1, mv1, b).then_inc(rstd1, 1)

            def rsqrt2(b):
                pool.wait_ge(var2, b + 1)
                rsqrt(rs2, mv2, b).then_inc(rstd2, 1)

            def views(t):
                return part[:, t % 4, NH:NQK], lambda a: a[:, t % 4].rearrange("p (h d) -> p h d", d=HD)

            def k_first(t):
                k, heads = views(t)
                pool.wait_ge(roped, t + 1)
                nc.gpsimd.tensor_copy(k[:, :, 1:6:2, :], heads(rq)[:, NH:NQK].unsqueeze(2).broadcast_to([P, NKV, 3, HD])
                                      ).then_inc(p0k_ready, 1)

            def k_rest(t):
                k, heads = views(t)
                pool.wait_ge(r1_ready, t + 1)
                nc.gpsimd.tensor_copy(k[:, :, 0:5:4, :], heads(r1)[:, NH:NQK].unsqueeze(2).broadcast_to([P, NKV, 2, HD])
                                      ).then_inc(p1k_ready, 1)
                pool.wait_ge(p1k_ready, t + 1)
                nc.gpsimd.tensor_tensor(k[:, :, 2, :], heads(r1)[:, NH:NQK], k[:, :, 4, :], ALU.subtract
                                        ).then_inc(k_parts, 1)

            def split(t):
                i = t % 4
                q, (k, heads) = part[:, i, 0:NH], views(t)
                pool.wait_ge(rope_prod, t + 1)
                nc.gpsimd.tensor_tensor(rq[:, i], ra[:, i], rb[:, i], ALU.add).then_inc(roped, 1)
                k_first(t)
                pool.wait_ge(p0k_ready, t + 1)
                pool.wait_ge(p0_ready, t + 1)
                nc.gpsimd.tensor_tensor(heads(r1), heads(rq), part[:, i, :, 1, :], ALU.subtract).then_inc(r1_ready, 1)
                k_rest(t)
                pool.wait_ge(p1_ready, t + 1)
                nc.gpsimd.tensor_tensor(q[:, :, 5, :], heads(r1)[:, 0:NH], q[:, :, 4, :], ALU.subtract
                                        ).then_inc(q_parts, 1)

            def ternary(i):
                if i == 0:
                    pool.wait_ge(scale_ready, 3)
                n, m = (HC, CH * D) if i < 2 else (P, KC * HP)
                src = (w1n, w3n, w2n)[i][:, :, :].rearrange("p c d -> p (c d)")
                chain(nc.gpsimd.tensor_scalar(tpos[0:n, 0:m], src, thr[0:n, i:i + 1], None, ALU.is_gt))
                chain(nc.gpsimd.tensor_scalar(tneg[0:n, 0:m], src, nthr[0:n, i:i + 1], None, ALU.is_lt))
                nc.gpsimd.tensor_tensor(tern[0:n, i, 0:m], tneg[0:n, 0:m], tpos[0:n, 0:m],
                                        ALU.subtract).then_inc(tern_ready, 1)
                pool.wait_ge(tern_ready, i + 1)

            def gate_lo(n):
                pool.wait_ge(ghi, n + 1)
                nc.gpsimd.tensor_tensor(gT[:, 1, n, :], g[:, n % 4, :], gT[:, 0, n, :],
                                        ALU.subtract).then_inc(glo, 1)

            rsqrt1(0)
            rsqrt1(1)
            k_first(0)
            k_first(1)
            k_rest(0)
            k_rest(1)
            rsqrt1(2)
            split(2)
            split(3)
            rsqrt1(3)
            for b in range(NB):
                if b >= 1:
                    rsqrt2(b - 1)
                if b + 2 < NB:
                    split(2 * b + 4)
                    split(2 * b + 5)
                if b < 3:
                    ternary(b)
            for n in range(NU):
                if n == 2 * CH + 2:
                    rsqrt2(NB - 1)
                gate_lo(n)

        @block.scalar
        def _(act):
            act.wait_ge(in_cst, 16)
            nc.scalar.activation(idb[:, :], id32, ACT.Copy).then_inc(idents, 1)
            nc.scalar.activation(idh[:, :], id32, ACT.Copy).then_inc(idents, 1)

            def evac_hT(t):
                act.wait_ge(hT_psum, t + 1)
                nc.scalar.activation(hT[:, t % 2].rearrange("p k n -> p (k n)"), bank(2 + t % 2, D), ACT.Copy).then_inc(hT_ready, 1)

            def evac_v(t):
                act.wait_ge(qkv_psum, t + 1)
                act.wait_ge(rope_prod, t + 1)
                if t == 0:
                    act.wait_ge(pool_init, 4)
                nc.scalar.activation(vst[:, t, :, 0:HD],
                                     bank(qkv_bank(t))[:, NQK * HD:QKV].rearrange("p (k d) -> p k d", d=HD),
                                     ACT.Copy).then_inc(v_ready, 1)

            def split0(t):
                act.wait_ge(roped, t + 1)
                src = rq[:, t % 4, 0:NH * HD].rearrange("p (h d) -> p h d", d=HD).unsqueeze(2)
                nc.scalar.activation(part[:, t % 4, 0:NH, 0:3, :], src.broadcast_to([P, NH, 3, HD]),
                                     ACT.Copy).then_inc(p0_ready, 1)

            def split1(t):
                act.wait_ge(r1_ready, t + 1)
                src = r1[:, t % 4, 0:NH * HD].rearrange("p (h d) -> p h d", d=HD).unsqueeze(2)
                nc.scalar.activation(part[:, t % 4, 0:NH, 3:5, :], src.broadcast_to([P, NH, 2, HD]),
                                     ACT.Copy).then_inc(p1_ready, 1)

            def evac_q(b, i):
                act.wait_ge(stack_psum, 5 * b + (1, 2, 4, 5)[i])
                half, qt = i % 2, i // 2
                nc.scalar.activation(qs[0:SLOT, b % 2, 8 * half:8 * half + 8, qt * P:(qt + 1) * P],
                                     ps[0:SLOT, i, :].bitcast(BF16).rearrange("p (h n) -> p h n", n=P),
                                     ACT.Copy).then_inc(stack_act, 1)

            def evac_oT(b, qt):
                act.wait_ge(oT_psum, 2 * b + qt + 1)
                nc.scalar.activation(oT[:, qt].rearrange("p k n -> p (k n)"), proj_bank(b, qt), ACT.Copy).then_inc(oT_ready, 1)

            def evac_ot(b, half):
                act.wait_ge(pv_done, 8 * b + 4 * half + 4)
                if b >= 1 and half == 0:
                    act.wait_ge(o_psum, 2 * b)
                nc.scalar.activation(ot[:, 2 * half:2 * half + 2, :].rearrange("p k s -> p (k s)"),
                                     bank(6), ACT.Copy).then_inc(ot_ready, 1)

            def exps(b, v):
                n = 8 * b + v
                act.wait_ge(score_psum, n + 1)
                if n >= 3:
                    act.wait_ge(pv_done, n - 2)
                src = ps[:, 2 * (n % 2):2 * (n % 2) + 2, :].rearrange("p a s -> p (a s)")
                nc.scalar.activation(pt[:, n % 3].rearrange("p r s -> p (r s)"), src, ACT.Exp,
                                     scale=float(HD) ** -0.5).then_inc(exp_done, 1)

            def split_h2(b, qt):
                t = 2 * b + qt
                act.wait_ge(h2T_psum, t + 1)
                nc.scalar.activation(h2T[:, 0, :, t * P:(t + 1) * P],
                                     h2_bank(b, qt), ACT.Copy).then_inc(h2hi, 1)

            def weight_sum(i):
                wn = (w1n, w3n, w2n)[i]
                n = HC if i < 2 else P
                act.wait_ge(in_w[i], 32 if i < 2 else 16)
                if i == 0:
                    act.wait_ge(dve_pad, 4)
                else:
                    act.wait_ge(wsum_ready, i)
                src = wn[:, :, :].rearrange("p c d -> p (c d)")
                nc.scalar.activation(wabs[0:n, 0:src.shape[1]], src, ACT.Abs,
                                     accum_out=wsum[0:n, i:i + 1]).then_inc(wsum_ready, 1)

            def evac_wT(w):
                for k in range(KC):
                    act.wait_ge(wT_psum, 2 * w + k + 1)
                    nc.scalar.activation((w1T, w3T)[w][:, k, :], bank(2 + k).bitcast(F16)[:, 0:HP], ACT.Copy,
                                         scale=1.0 if w == 0 else W3SHIFT).then_inc(wT_act, 1)

            def tanh(n):
                act.wait_ge(up_psum, n + 1)
                if n == 0:
                    act.wait_ge(scale_ready, 4)
                if n >= 4:
                    act.wait_ge(g_ready, n - 3)
                nc.scalar.activation(u[:, n % 4, :], ps[0:HC, up_bank(n), 0:S], ACT.Tanh,
                                     scale=sgate[0:HC, :]).then_inc(tanh_done, 1)

            def gate_hi(n):
                act.wait_ge(g_ready, n + 1)
                nc.scalar.activation(gT[:, 0, n, :], g[:, n % 4, :], ACT.Copy).then_inc(ghi, 1)

            evac_hT(0)
            evac_hT(1)
            evac_v(0)
            split0(0)
            evac_hT(2)
            evac_hT(3)
            evac_v(1)
            split0(1)
            split1(0)
            split1(1)
            evac_v(2)
            evac_q(0, 0)
            split0(2)
            evac_q(0, 2)
            split1(2)
            weight_sum(0)
            evac_v(3)
            evac_hT(4)
            evac_hT(5)
            split0(3)
            split1(3)
            evac_q(1, 0)
            weight_sum(1)
            evac_q(1, 2)
            weight_sum(2)
            for b in range(NB):
                t = 2 * b + 4
                if 1 <= b and t < NT:
                    evac_hT(t)
                    evac_hT(t + 1)
                if b >= 2:
                    evac_wT(b - 2)
                if b >= 1:
                    evac_oT(b - 1, 0)
                    evac_oT(b - 1, 1)
                for v in range(8):
                    if b < NB - 1:
                        exps(b, v)
                    else:
                        for n in range(first_unit(v), first_unit(v + 1)):
                            tanh(n)
                            if n == first_unit(v):
                                exps(b, v)
                            if n >= 1:
                                gate_hi(n - 1)
                    if b < 2:
                        if v == b:
                            evac_v(t)
                        if v == 1:
                            split0(t)
                        if v == 2:
                            split1(t)
                        if v == 1 + 2 * b:
                            evac_v(t + 1)
                        if v == 3 + b:
                            split0(t + 1)
                        if v == 5 + b:
                            split1(t + 1)
                    if v == 4:
                        evac_ot(b, 0)
                    if b >= 1 and v == (3 if b == NB - 1 else 4):
                        split_h2(b - 1, 0)
                    if b >= 1 and v == (5 if b == NB - 1 else 6):
                        split_h2(b - 1, 1)
                evac_ot(b, 1)
                if b + 2 < NB:
                    evac_q(b + 2, 0)
                    evac_q(b + 2, 2)
            b, n = NB - 1, 2 * CH
            gate_hi(n - 1)
            tanh(n)
            evac_oT(b, 0)
            evac_oT(b, 1)
            gate_hi(n)
            for i in range(1, 4):
                tanh(n + i)
                gate_hi(n + i)
            split_h2(b, 0)
            split_h2(b, 1)
            tanh(n + 4)
            for n in range(2 * CH + 5, NU):
                tanh(n)
                gate_hi(n - 1)
            gate_hi(NU - 1)

        @block.vector
        def _(dve):
            nc.vector.memset(w1n[96:HC, CH - 1, :], 0.0).then_inc(dve_pad, 1)
            nc.vector.memset(w3n[96:HC, CH - 1, :], 0.0).then_inc(dve_pad, 1)
            nc.vector.memset(w2n[:, :, HID:HP], 0.0).then_inc(dve_pad, 1)
            nc.vector.memset(wsum[:, :], 0.0).then_inc(dve_pad, 1)
            steps = [0]

            def chain(ins):
                steps[0] += 1
                ins.then_inc(dve_step, 1)
                dve.wait_ge(dve_step, steps[0])

            def stats(src, st, mv, b, signal):
                for qt in range(2):
                    ins = nc.vector.bn_stats(st[:, 2 * b + qt, :], src[:, 2 * b + qt, :])
                    ins.then_inc(dve_step, 1)
                    steps[0] += 1
                dve.wait_ge(dve_step, steps[0])
                for qt in range(2):
                    last = nc.vector.bn_aggr(mv[:, 2 * b + qt, :], st[:, 2 * b + qt, :])
                    if qt == 0:
                        last.then_inc(dve_step, 1)
                        steps[0] += 1
                last.then_inc(signal, 1)

            def norm1(b):
                dve.wait_ge(rstd1, b + 1)
                for qt in range(2):
                    t = 2 * b + qt
                    nc.vector.tensor_scalar(hn[:, t, :], x_sb[:, t, :], mv1[:, t, 0:1], rs1[:, t, 1:2],
                                            ALU.subtract, ALU.mult).then_inc(normed1, 1)

            def rope(t):
                i, qt = t % 4, t % 2
                if t == 0:
                    dve.wait_ge(in_cst, 16)
                dve.wait_ge(qkv_psum, t + 1)
                qk = bank(qkv_bank(t))[:, 0:NQK * HD].rearrange("p (h f e) -> p h f e", f=HD // 2, e=2)
                c = cos[:, qt].unsqueeze(1).broadcast_to([P, NQK, HD])
                s = sin[:, qt].rearrange("p (f e) -> p f e", e=2).unsqueeze(1).broadcast_to([P, NQK, HD // 2, 2])
                nc.vector.tensor_tensor(ra[:, i].rearrange("p (h d) -> p h d", d=HD),
                                        bank(qkv_bank(t))[:, 0:NQK * HD].rearrange("p (h d) -> p h d", d=HD), c,
                                        ALU.mult)
                nc.vector.tensor_tensor(rb[:, i].rearrange("p (h f e) -> p h f e", f=HD // 2, e=2), qk[:, :, :, ::-1], s,
                                        ALU.mult).then_inc(rope_prod, 1)

            def rope_sum(t):
                dve.wait_ge(rope_prod, t + 1)
                nc.vector.tensor_tensor(rq[:, t], ra[:, t], rb[:, t], ALU.add).then_inc(roped, 1)

            def remainder(t):
                heads = lambda a: a[:, t].rearrange("p (h d) -> p h d", d=HD)
                dve.wait_ge(roped, t + 1)
                dve.wait_ge(p0_ready, t + 1)
                dve.wait_ge(p0k_ready, t + 1)
                nc.vector.tensor_tensor(heads(r1), heads(rq), part[:, t, :, 1, :], ALU.subtract).then_inc(r1_ready, 1)

            def third_part(t):
                dve.wait_ge(r1_ready, t + 1)
                dve.wait_ge(p1_ready, t + 1)
                nc.vector.tensor_tensor(part[:, t, 0:NH, 5, :], r1[:, t, 0:NH * HD].rearrange("p (h d) -> p h d", d=HD),
                                        part[:, t, 0:NH, 4, :], ALU.subtract).then_inc(q_parts, 1)

            def evac_q(b, i):
                dve.wait_ge(stack_psum, 5 * b + (1, 2, 4, 5)[i])
                half, qt = i % 2, i // 2
                nc.vector.tensor_copy(qs[0:SLOT, b % 2, 8 * half:8 * half + 8, qt * P:(qt + 1) * P],
                                      ps[0:SLOT, i, :].bitcast(BF16).rearrange("p (h n) -> p h n", n=P)
                                      ).then_inc(stack_dve, 1)

            def evac_k(b):
                dve.wait_ge(stack_psum, 5 * b + 3)
                nc.vector.tensor_copy(ks[0:SLOT, b % 2, :, :].rearrange("p k s -> p (k s)"),
                                      ps[0:SLOT, 7, :].bitcast(BF16)).then_inc(stack_dve, 1)

            def row_max(b, w):
                qt, kv, rp = w // 8, (w // 2) % 4, w % 2
                dve.wait_ge(max_psum, 16 * b + w + 1)
                if w == 0 and b >= 1:
                    dve.wait_ge(nms_ready, b)
                nc.vector.tensor_reduce(nmx[:, qt, 2 * rp * NKV + kv:(2 * rp + 1) * NKV + kv + 1:NKV],
                                        bank(4 + w % 2).rearrange("p (r s) -> p r s", r=2),
                                        axis=AX.X, op=ALU.max, negate=True).then_inc(max_done, 1)

            def split_max(b):
                dve.wait_ge(max_done, 16 * b + 16)
                if b >= 1:
                    dve.wait_ge(nmT_psum, b)
                chain(nc.vector.tensor_copy(nms[:, :, 0, :], nmx[:, :, :]))
                chain(nc.vector.tensor_tensor(nmr[:, :, :], nmx[:, :, :], nms[:, :, 0, :], ALU.subtract))
                chain(nc.vector.tensor_copy(nms[:, :, 1, :], nmr[:, :, :]))
                nc.vector.tensor_tensor(nms[:, :, 2, :], nmr[:, :, :], nms[:, :, 1, :],
                                        ALU.subtract).then_inc(nms_ready, 1)

            def evac_max(b):
                dve.wait_ge(nmT_psum, b + 1)
                if b >= 2:
                    dve.wait_ge(mrows, 16 * MROW * (b - 1))
                nc.vector.tensor_copy(nmT[:, b % 2, :], ps[0:MROW * NH, 5, 0:S // 2].bitcast(BF16)).then_inc(nmT_ready, 1)

            def normalise(b, qt):
                dve.wait_ge(o_psum, 2 * b + qt + 1)
                if b >= 1:
                    dve.wait_ge(oT_psum, 2 * b - 1 + qt)
                o = bank(qt).rearrange("p (k r c) -> p k r c", k=NKV, r=REP)
                rd = rden[:, qt].rearrange("p (k r) -> p k r", k=NKV)
                chain(nc.vector.reciprocal(rd, o[:, :, :, HD]))
                nc.vector.tensor_tensor(on[:, qt].rearrange("p r k d -> p k r d"), o[:, :, :, 0:HD],
                                        rd.unsqueeze(3).broadcast_to([P, NKV, REP, HD]),
                                        ALU.mult).then_inc(on_ready, 1)

            def residual(b, qt):
                t = 2 * b + qt
                dve.wait_ge(wo_psum, t + 1)
                nc.vector.tensor_tensor(x1[:, t, :], x_sb[:, t, :], proj_bank(b, qt), ALU.add).then_inc(x1_ready, 1)

            def norm2(b):
                dve.wait_ge(rstd2, b + 1)
                for qt in range(2):
                    t = 2 * b + qt
                    if b >= 1:
                        dve.wait_ge(h2T_psum, t - 1)
                    nc.vector.tensor_scalar(h2[:, qt, :], x1[:, t, :], mv2[:, t, 0:1], rs2[:, t, 1:2],
                                            ALU.subtract, ALU.mult).then_inc(h2_ready, 1)

            def split_h2(b, qt):
                t = 2 * b + qt
                dve.wait_ge(h2hi, t + 1)
                sl = slice(t * P, (t + 1) * P)
                nc.vector.tensor_tensor(h2T[:, 1, :, sl], h2_bank(b, qt),
                                        h2T[:, 0, :, sl], ALU.subtract).then_inc(h2lo, 1)

            def layer_norm2_stats(b):
                dve.wait_ge(x1_ready, 2 * b + 2)
                stats(x1, st2, mv2, b, var2)

            def scales():
                dve.wait_ge(wtot_psum, 1)
                nc.vector.tensor_scalar(scl[:, :], bank(4, 3), 1.0 / (HID * D), None, ALU.mult).then_inc(scale_ready, 1)
                dve.wait_ge(scale_ready, 1)
                nc.vector.tensor_scalar(thr[:, :], scl[:, :], 0.5, None, ALU.mult).then_inc(scale_ready, 1)
                nc.vector.tensor_scalar(nthr[:, :], scl[:, :], -0.5, None, ALU.mult).then_inc(scale_ready, 1)
                nc.vector.tensor_scalar(sgate[:, :], scl[:, 0:1], -0.5, None, ALU.mult).then_inc(scale_ready, 1)
                chain(nc.vector.tensor_tensor(sout[:, 0:1], scl[:, 0:1], scl[:, 1:2], ALU.mult))
                chain(nc.vector.scalar_tensor_tensor(sout[:, 1:2], sout[:, 0:1], -0.5 / W3SHIFT, scl[:, 2:3],
                                                     ALU.mult, ALU.mult))

            def evac_w2T():
                for k in range(KC):
                    dve.wait_ge(wT_psum, 4 + k + 1)
                    nc.vector.tensor_copy(w2T[:, :, k * P:(k + 1) * P],
                                          ps[0:HC, 4 + k, :].bitcast(F16)[:, 0:CH * P].rearrange("p (c n) -> p c n", c=CH)
                                          ).then_inc(wT_dve, 1)

            def gate(n):
                yb = ps[0:HC, up_bank(n), :]
                dve.wait_ge(tanh_done, n + 1)
                if n >= 4:
                    dve.wait_ge(glo, n - 3)
                chain(nc.vector.scalar_tensor_tensor(uv[:, n % 4, :], u[:, n % 4, :], 1.0, yb[:, 0:S],
                                                     ALU.add, ALU.mult))
                nc.vector.tensor_tensor(g[:, n % 4, :], uv[:, n % 4, :], yb[:, S:2 * S], ALU.mult).then_inc(g_ready, 1)

            def output(n):
                dve.wait_ge(down_psum, n + 1)
                t = 2 * n if n < NB - 1 else NB - 1 + n
                e = t + 2 if n < NB - 1 else t + 1
                src = ps[:, (7, 2, 7, 2, 1)[n], 0:(e - t) * D].rearrange("p (t d) -> p t d", d=D)
                nc.vector.scalar_tensor_tensor(y[:, t:e, :], src, sout[:, 1:2], x1[:, t:e, :],
                                               ALU.mult, ALU.add).then_inc(y_ready, 1)

            for b in range(2):
                dve.wait_ge(in_x[b], 16)
                stats(x_sb, st1, mv1, b, var1)
                norm1(b)
            for t in range(2):
                rope(t)
                rope_sum(t)
            remainder(0)
            remainder(1)
            third_part(0)
            rope(2)
            third_part(1)
            dve.wait_ge(in_x[2], 16)
            stats(x_sb, st1, mv1, 2, var1)
            evac_q(0, 1)
            evac_k(0)
            evac_q(0, 3)
            for w in range(16):
                row_max(0, w)
                if w == 1:
                    rope(3)
                if w == 3:
                    norm1(2)
                if w == 7:
                    dve.wait_ge(in_x[3], 16)
                    stats(x_sb, st1, mv1, 3, var1)
                if w == 11:
                    evac_q(1, 1)
                if w == 13:
                    evac_k(1)
                if w == 15:
                    evac_q(1, 3)
            split_max(0)
            evac_max(0)

            for b in range(NB):
                t = 2 * b + 4
                if b >= 1:
                    normalise(b - 1, 0)
                    normalise(b - 1, 1)
                if b == 0:
                    rope(4)
                    scales()
                if b == NB - 1:
                    evac_w2T()
                lead = MAX_LEAD[b] if b + 1 < NB else 0
                for w in range(0, lead):
                    if b >= 1 and w >= 2:
                        residual(b - 1, w - 2)
                    row_max(b + 1, w)
                if b >= 1:
                    for qt in range(max(lead - 2, 0), 2):
                        residual(b - 1, qt)
                for v in range(8):
                    if b + 1 < NB:
                        for w in max_units(b, v):
                            row_max(b + 1, w)
                            if w == 15:
                                split_max(b + 1)
                    if v == 0 and b == 0:
                        rope(5)
                    if v in (0, 2) and b == 1:
                        rope(6 + v // 2)
                    if b >= 1 and v == 0:
                        layer_norm2_stats(b - 1)
                    if b >= 1 and v == (2 if b < NB - 1 else 1):
                        norm2(b - 1)
                    if b == 0 and v == 1:
                        norm1(3)
                    if b == NB - 1:
                        for n in range(first_unit(v), first_unit(v + 1)):
                            gate(n)
                    if b >= 1 and v == (3 if b == NB - 1 else 5):
                        split_h2(b - 1, 0)
                    if b >= 1 and v == (5 if b == NB - 1 else 7):
                        split_h2(b - 1, 1)
                if b + 1 < NB:
                    evac_max(b + 1)
                if b + 2 < NB:
                    evac_q(b + 2, 1)
                    evac_k(b + 2)
                    evac_q(b + 2, 3)
            b, n = NB - 1, 2 * CH
            normalise(b, 0)
            normalise(b, 1)
            output(0)
            gate(n)
            gate(n + 1)
            residual(b, 0)
            residual(b, 1)
            layer_norm2_stats(b)
            gate(n + 2)
            norm2(b)
            gate(n + 3)
            output(1)
            split_h2(b, 0)
            split_h2(b, 1)
            for n in range(2 * CH + 4, NU):
                gate(n)
                if n == NU - 2:
                    output(2)
            output(3)
            output(4)

        @block.tensor
        def _(pe):
            def tr_h(t):
                pe.wait_ge(normed1, t + 1)
                if t == 0:
                    pe.wait_ge(in_cst, 16)
                if t >= 2:
                    pe.wait_ge(hT_ready, t - 1)
                for k in range(KC):
                    last = nc.tensor.transpose(bank(2 + t % 2)[:, k * P:(k + 1) * P], hn[:, t, k * P:(k + 1) * P], id32)
                last.then_inc(hT_psum, 1)

            def project(t):
                pe.wait_ge(hT_ready, t + 1)
                if t == 0:
                    pe.wait_ge(in_wqkv, 48)
                if t >= 2:
                    pe.wait_ge(v_ready, t - 1 if t < 6 else t)
                if t == 6:
                    pe.wait_ge(x1_ready, 2)
                if t in (3, 5, 6):
                    pe.wait_ge(stack_dve, 3 * (t // 2 - 1) + 2)
                for k in range(KC):
                    last = nc.tensor.matmul(bank(qkv_bank(t), QKV), hT[:, t % 2, k, :], wqkv_sb[:, k, :],
                                            start=(k == 0), stop=(k == KC - 1))
                last.then_inc(qkv_psum, 1)

            def stack_q(b, i):
                half, qt = i % 2, i // 2
                t = 2 * b + qt
                pe.wait_ge(q_parts, t + 1)
                if t == 0:
                    pe.wait_ge(idents, 1)
                dst = ps[0:SLOT, i, :].bitcast(BF16)
                for j in range(8):
                    last = nc.tensor.transpose(dst[:, j * P:(j + 1) * P],
                                               part[:, t % 4, 8 * half + j].rearrange("p s d -> p (s d)"), idb[:, :])
                last.then_inc(stack_psum, 1)

            def stack_k(b):
                pe.wait_ge(k_parts, 2 * b + 2)
                if b == 0:
                    pe.wait_ge(idents, 1)
                dst = ps[0:SLOT, 7, :].bitcast(BF16)
                for kv in range(NKV):
                    for kt in range(2):
                        j = 2 * kv + kt
                        last = nc.tensor.transpose(dst[:, j * P:(j + 1) * P],
                                                   part[:, (2 * b + kt) % 4, NH + kv].rearrange("p s d -> p (s d)"), idb[:, :])
                last.then_inc(stack_psum, 1)

            def max_scores(b, w):
                qt, kv, rp = w // 8, (w // 2) % 4, w % 2
                n = 16 * b + w
                if w % 8 == 0:
                    pe.wait_ge(stack_act, 2 * b + 1 + w // 8)
                    pe.wait_ge(stack_dve, 3 * b + 2 + w // 8)
                if w == 0 and b >= 1:
                    pe.wait_ge(nmT_ready, b)
                if n == 16:
                    pe.wait_ge(scale_ready, 1)
                if n >= 2:
                    pe.wait_ge(max_done, n - 1)
                for r in range(2):
                    last = nc.tensor.matmul(bank(4 + w % 2)[:, r * S:(r + 1) * S],
                                            qs[0:SLOT, b % 2, (2 * rp + r) * NKV + kv, qt * P:(qt + 1) * P],
                                            ks[0:SLOT, b % 2, kv, :], start=True, stop=True)
                last.then_inc(max_psum, 1)

            def scores(b, v):
                n, kv, kt = 8 * b + v, v // 2, v % 2
                if v == 0:
                    pe.wait_ge(mrows, 16 * MROW * (b + 1))
                    pe.wait_ge(pool_init, 5)
                if v == 0:
                    pe.wait_ge(stack_act, 2 * min(b + 2, NB))
                    pe.wait_ge(stack_dve, 3 * min(b + 2, NB))
                    pe.wait_ge(hT_ready, min(2 * b + 6, NT))
                    if b >= 1:
                        pe.wait_ge(on_ready, 2 * b)
                if b >= 2 and v == 1:
                    pe.wait_ge(wT_act, 2 * (b - 1))
                if n >= 2:
                    pe.wait_ge(exp_done, n - 1)
                for h in range(2):
                    last = nc.tensor.matmul(bank(2 * (n % 2) + h), ks[0:SLOT + MROW, b % 2, kv, kt * P:(kt + 1) * P],
                                            qs[0:SLOT + MROW, b % 2, 2 * h * NKV + kv:(2 * h + 1) * NKV + kv + 1:NKV, :],
                                            start=True, stop=True)
                last.then_inc(score_psum, 1)

            def pv(b, v):
                n, kv, kt = 8 * b + v, v // 2, v % 2
                pe.wait_ge(exp_done, n + 1)
                if v == 0:
                    pe.wait_ge(v_ready, max(2 * b + 2, 5))
                    if b >= 1:
                        pe.wait_ge(ot_ready, 2 * b)
                        pe.wait_ge(x1_ready, 2 * b - 1)
                if v == 4:
                    pe.wait_ge(ot_ready, 2 * b + 1)
                for r in range(REP):
                    last = nc.tensor.matmul(ps[VW * r:VW * (r + 1), 6, (kv % 2) * S:(kv % 2 + 1) * S],
                                            vst[:, 2 * b + kt, kv, :], pt[:, n % 3, r, :],
                                            start=(kt == 0), stop=(kt == 1))
                last.then_inc(pv_done, 1)

            def tr_max(b):
                pe.wait_ge(nms_ready, b + 1)
                dst = ps[0:MROW * NH, 5, 0:S // 2].bitcast(BF16)
                for qt in range(2):
                    last = nc.tensor.transpose(dst[:, qt * P:(qt + 1) * P], nms[:, qt].rearrange("p m h -> p (m h)"), idb[:, :])
                last.then_inc(nmT_psum, 1)

            def tr_o(b, qt):
                if qt == 0:
                    pe.wait_ge(ot_ready, 2 * b + 2)
                    if b + 2 < NB:
                        pe.wait_ge(stack_act, 2 * (b + 2) + 1)
                        pe.wait_ge(stack_dve, 3 * (b + 2) + 1)
                for kv in range(NKV):
                    last = nc.tensor.transpose(bank(qt)[:, kv * P:(kv + 1) * P], ot[:, kv, qt * P:(qt + 1) * P], id32)
                last.then_inc(o_psum, 1)

            def tr_on(b, qt):
                pe.wait_ge(on_ready, 2 * b + qt + 1)
                if b < NB - 1 and qt == 1:
                    pe.wait_ge(v_ready, min(6 + 2 * b, 8) if b else 6)
                    pe.wait_ge(stack_dve, 3 * min(b + 3, NB))
                    if b >= 1:
                        pe.wait_ge(h2lo, 2 * b)
                o = on[:, qt].rearrange("p r k d -> p (r k d)")
                for k in range(KC):
                    last = nc.tensor.transpose(proj_bank(b, qt)[:, k * P:(k + 1) * P], o[:, k * P:(k + 1) * P], id32)
                last.then_inc(oT_psum, 1)

            def out_proj(b, qt):
                pe.wait_ge(oT_ready, 2 * b + qt + 1)
                if b == 0 and qt == 0:
                    pe.wait_ge(in_wo, 16)
                for k in range(KC):
                    last = nc.tensor.matmul(proj_bank(b, qt), oT[:, qt, k, :], wo_sb[:, k, :],
                                            start=(k == 0), stop=(k == KC - 1))
                last.then_inc(wo_psum, 1)

            def tr_h2(b, qt):
                pe.wait_ge(h2_ready, 2 * b + qt + 1)
                for k in range(KC):
                    last = nc.tensor.transpose(h2_bank(b, qt)[:, k, :], h2[:, qt, k * P:(k + 1) * P], id32)
                last.then_inc(h2T_psum, 1)

            def tr_w(w, k, bk):
                pe.wait_ge(tern_ready, w + 1)
                for c in range(CH):
                    if w < 2:
                        last = nc.tensor.transpose(bank(bk).bitcast(F16)[:, c * HC:(c + 1) * HC],
                                                   tern[0:HC, w, c * D + k * P:c * D + (k + 1) * P], idh[0:HC, 0:HC])
                    else:
                        last = nc.tensor.transpose(ps[0:HC, bk, :].bitcast(F16)[:, c * P:(c + 1) * P],
                                                   tern[:, 2, k * HP + c * HC:k * HP + (c + 1) * HC], idh[:, :])
                last.then_inc(wT_psum, 1)

            def up(n):
                f, c = n // CH, n % CH
                if c == 0:
                    pe.wait_ge(h2lo, 2 * f + 2)
                if n == 0:
                    pe.wait_ge(wT_act, 4)
                    pe.wait_ge(wT_dve, 2)
                if 2 <= n < WIDE + 2:
                    pe.wait_ge(g_ready, n - 1)
                if n == WIDE + 2:
                    pe.wait_ge(x1_ready, 2 * NB)
                if n >= WIDE + 4:
                    pe.wait_ge(g_ready, n - 3)
                for m, wT in enumerate((w1T, w3T)):
                    for i in range(2 * KC):
                        k, part_ = i // 2, i % 2
                        last = nc.tensor.matmul(ps[0:HC, up_bank(n), m * S:(m + 1) * S], wT[:, k, c * HC:(c + 1) * HC],
                                                h2T[:, part_, k, f * S:(f + 1) * S],
                                                start=(i == 0), stop=(i == 2 * KC - 1))
                last.then_inc(up_psum, 1)

            def down_chunk(t, c):
                f, j = t // 2, t % 2
                for h in range(2):
                    last = nc.tensor.matmul(down_bank(t), gT[:, h, f * CH + c, j * P:(j + 1) * P], w2T[:, c, :],
                                            start=(c == 0 and h == 0), stop=(c == CH - 1 and h == 1))
                return last

            def down(t):
                pe.wait_ge(glo, CH * (t // 2 + 1))
                if t == 0:
                    pe.wait_ge(wT_dve, 2)
                    pe.wait_ge(h2lo, 2 * NB - 2)
                if t == 4:
                    pe.wait_ge(y_ready, 1)
                for c in range(CH):
                    last = down_chunk(t, c)
                if t % 2:
                    last.then_inc(down_psum, 1)

            def stack_group(b, j):
                if j == 2:
                    stack_k(b)
                else:
                    stack_q(b, (0, 1, None, 2, 3)[j])

            pe.wait_ge(pool_init, 1)
            for _ in range(WARM):
                nc.tensor.matmul(bank(0, P), ones.bitcast(BF16)[:, 0:P], ones.bitcast(BF16)[:, 0:P], start=True, stop=True)
            tr_h(0)
            tr_h(1)
            project(0)
            project(1)
            tr_h(2)
            tr_h(3)
            project(2)
            pe.wait_ge(hT_ready, 4)
            pe.wait_ge(v_ready, 2)
            for j in range(5):
                stack_group(0, j)
            for w in range(16):
                max_scores(0, w)
                if w == 1:
                    project(3)
                if w == 7:
                    pe.wait_ge(stack_act, 2)
                    pe.wait_ge(stack_dve, 3)
                    tr_h(4)
                    tr_h(5)
                if w == 11:
                    project(4)
                if w in (9, 10, 12, 13, 14):
                    if w == 9:
                        pe.wait_ge(stack_act, 2)
                        pe.wait_ge(stack_dve, 3)
                    if w == 12:
                        pe.wait_ge(v_ready, 4)
                    if w == 13:
                        pe.wait_ge(hT_ready, 6)
                    stack_group(1, (9, 10, 12, 13, 14).index(w))
            tr_max(0)

            for b in range(NB):
                t = 2 * b + 4
                if b >= 1:
                    tr_o(b - 1, 0)
                    tr_o(b - 1, 1)
                if 1 <= b and t < NT:
                    pe.wait_ge(stack_act, 2 * (b + 2))
                    pe.wait_ge(stack_dve, 3 * (b + 2))
                    tr_h(t)
                    tr_h(t + 1)
                if b == 0:
                    pe.wait_ge(wsum_ready, 3)
                    pe.wait_ge(pool_init, 5)
                    pe.wait_ge(max_done, 16)
                    nc.tensor.matmul(bank(4, 3), ones[:, :], wsum[:, :], start=True, stop=True).then_inc(wtot_psum, 1)
                    for w in range(MAX_LEAD[0]):
                        max_scores(1, w)
                if b == 2:
                    pe.wait_ge(idents, 2)
                if b >= 2:
                    pe.wait_ge(exp_done, 8 * b)
                    pe.wait_ge(stack_act, 2 * NB)
                    pe.wait_ge(stack_dve, 3 * NB)
                    tr_w(b - 2, 0, 2)
                    tr_w(b - 2, 1, 3)
                if b == NB - 1:
                    pe.wait_ge(max_done, 16 * NB)
                    pe.wait_ge(nmT_ready, NB)
                    tr_w(2, 0, 4)
                    tr_w(2, 1, 5)
                if b >= 1:
                    for w in range(4):
                        if b + 1 < NB and w < MAX_LEAD[b]:
                            max_scores(b + 1, w)
                        if w < 2:
                            tr_on(b - 1, w)
                        else:
                            out_proj(b - 1, w - 2)
                for v in range(8):
                    scores(b, v)
                    if b + 1 < NB:
                        for w in max_units(b, v):
                            max_scores(b + 1, w)
                    if v == 0 and b == 0:
                        project(5)
                    if v in (0, 2) and b == 1:
                        project(6 + v // 2)
                    if b == NB - 1:
                        for n in range(first_unit(v), first_unit(v + 1)):
                            up(n)
                    if v >= 1:
                        pv(b, v - 1)
                    if b >= 1 and v == (2 if b == NB - 1 else 4):
                        pe.wait_ge(v_ready, min(2 * b + 6, NT))
                        pe.wait_ge(stack_dve, 3 * min(b + 2, NB))
                        if b >= 2:
                            pe.wait_ge(h2lo, 2 * b - 2)
                        tr_h2(b - 1, 0)
                    if b >= 1 and v == (4 if b == NB - 1 else 6):
                        pe.wait_ge(h2lo, 2 * b - 1)
                        tr_h2(b - 1, 1)
                    if b == NB - 1 and v >= 6:
                        down(v - 6)
                    if v == 7 and b + 1 < NB:
                        tr_max(b + 1)
                pv(b, 7)
                if b + 2 < NB:
                    pe.wait_ge(exp_done, 8 * b + 8)
                    if b >= 1:
                        pe.wait_ge(h2lo, 2 * b)
                    else:
                        pe.wait_ge(v_ready, 6)
                    for j in range(5):
                        stack_group(b + 2, j)
            b, n = NB - 1, 2 * CH
            tr_o(b, 0)
            tr_o(b, 1)
            up(n)
            tr_on(b, 0)
            tr_on(b, 1)
            up(n + 1)
            out_proj(b, 0)
            out_proj(b, 1)
            up(n + 2)
            down(2)
            up(n + 3)
            down(3)
            tr_h2(b, 0)
            tr_h2(b, 1)
            up(n + 4)
            up(n + 5)
            up(n + 6)
            up(n + 7)
            up(n + 8)
            down(4)
            up(n + 9)
            down(5)
            pe.wait_ge(y_ready, 2)
            pe.wait_ge(h2lo, 2 * NB)
            for c in range(CH):
                if c < 2:
                    up(n + 10 + c)
                pe.wait_ge(glo, 3 * CH + c + 1)
                for t in (6, 7):
                    last = down_chunk(t, c)
                    if c == CH - 1:
                        last.then_inc(down_psum, 1)


_W = ("L0_attn_W_q", "L0_attn_W_k", "L0_attn_W_v", "L0_attn_W_o", "L0_ffn_w1", "L0_ffn_w3", "L0_ffn_w2")


def _constants():
    half = HD // 2
    freq = (np.float32(1.0) / np.float32(10000.0) ** (np.arange(half, dtype=np.float32) / np.float32(half))).astype(np.float32)
    ang = np.arange(S, dtype=np.float32)[:, None] * freq[None, :]
    c, s = np.cos(ang).astype(np.float32), np.sin(ang).astype(np.float32)
    cos = np.repeat(c, 2, axis=1)
    sin = np.stack([-s, s], axis=-1).reshape(S, HD)
    tiles = [a.reshape(2, P, HD).transpose(1, 0, 2).reshape(P, 2 * HD) for a in (cos, sin)]
    return np.ascontiguousarray(np.concatenate([np.eye(P, dtype=np.float32), *tiles], axis=1))


def kernel(**inputs):
    import concourse.bacc as bacc
    from concourse.bass_utils import run_bass_kernel_spmd

    nc = bacc.Bacc("TRN2", target_bir_lowering=False, num_devices=1)
    arrays = {"x": np.ascontiguousarray(inputs["L0_attn_x"]), "consts": _constants()}
    for name in _W:
        arrays[name] = np.ascontiguousarray(inputs[name])
    aps = {n: nc.dram_tensor(n, a.shape, mybir.dt.from_np(a.dtype), kind="ExternalInput").ap() for n, a in arrays.items()}
    out = nc.dram_tensor("out", (NB, S, D), F32, kind="ExternalOutput").ap()
    w = [aps[n] for n in _W]
    build(nc, aps["x"], w[0:3], w[3], w[4], w[5], w[6], aps["consts"], out)
    r = run_bass_kernel_spmd(nc, [arrays], core_ids=[0])
    return r.results[0]["out"]
```
